# Optimizing a Trainium2 kernel written in Bass

```python
import numpy as np
import jax
import jax.numpy as jnp

def _softmax(x, axis=-1):
    return jax.nn.softmax(x, axis=axis)

def _gelu(x):
    return jax.nn.gelu(x, approximate=True)

def _silu(x):
    return jax.nn.silu(x)

def _sigmoid(x):
    return jax.nn.sigmoid(x)

def _layernorm(x, axis=-1, eps=1e-05):
    m = jnp.mean(x, axis=axis, keepdims=True)
    v = jnp.var(x, axis=axis, keepdims=True)
    return (x - m) / jnp.sqrt(v + eps)

def _scatter_add(tgt, idx, src, axis=0):
    return tgt.at[idx].add(src)

def _segment_sum(src, seg, n):
    return jax.ops.segment_sum(src, seg, n)
kernel_name = 'mk_audio_tower_d2_tok_audfeat512_r4_27d2d0'

def setup_inputs(seed: int=0):
    np.random.seed(seed)
    _w = jnp.asarray

    def _rec_inputs():
        import jax
        import jax.numpy as jnp
        _rk = jax.random.key(seed)
        x = -0.000292821 + 1.00034 * jax.random.normal(jax.random.fold_in(_rk, 1), (64, 375, 2), jnp.float32)
        return x
    x = _rec_inputs()

    def _L0_tok_setup():
        import jax, jax.numpy as jnp
        import numpy as np
        PATCH_LENGTH = 128
        PATCH_STRIDE = 64
        MODEL_DIM = 128
        LN_EPS = 0.001
        key = jax.random.key(seed)
        k1, k2 = jax.random.split(key)
        B, T, C = (64, 8192, 2)
        x = jax.random.normal(k1, (B, T, C), dtype=jnp.float32)
        in_dim = PATCH_LENGTH * C
        W = jax.random.normal(k2, (in_dim, MODEL_DIM), dtype=jnp.float32) / np.sqrt(in_dim)
        b = jnp.zeros((MODEL_DIM,), dtype=jnp.float32)
        gamma = jnp.ones((MODEL_DIM,), dtype=jnp.float32)
        beta = jnp.zeros((MODEL_DIM,), dtype=jnp.float32)
        return {'x': x, 'W': W, 'b': b, 'gamma': gamma, 'beta': beta}
    _L0_tok_all = _L0_tok_setup()
    _L0_tok_in = {k: v for k, v in _L0_tok_all.items() if k in ('W', 'b', 'gamma', 'beta')}
    del _L0_tok_all

    def _L0_attn_setup():
        import jax, jax.numpy as jnp
        import numpy as np
        key = jax.random.key(seed)
        k1, k2 = jax.random.split(key)
        x = jax.random.normal(k1, (4, 512, 128), dtype=jnp.float32)
        proxy = jax.random.normal(k2, (16, 128), dtype=jnp.float32)
        return {'x': x, 'proxy': proxy}
    _L0_attn_all = _L0_attn_setup()
    _L0_attn_in = {k: v for k, v in _L0_attn_all.items() if k in ('proxy',)}
    del _L0_attn_all

    def _L0_ffn_setup():
        import jax, jax.numpy as jnp
        import numpy as np
        N_DIM = 128
        HEADS = 8
        NUM_EXPERTS = 16384
        NUM_KEYS = 64
        DIM_KEY = 64
        TOPK = 16
        SCALE = 0.02
        key = jax.random.key(seed)
        k0, k1, k2, k3, k4 = jax.random.split(key, 5)
        x = jax.random.normal(k0, (1, 512, N_DIM), dtype=jnp.float32)
        W_q = jax.random.normal(k1, (N_DIM, 2 * HEADS * DIM_KEY), dtype=jnp.float32) * SCALE
        keys = jax.random.normal(k2, (HEADS, NUM_KEYS, 2, DIM_KEY), dtype=jnp.float32) * SCALE
        down_embed = jax.random.normal(k3, (NUM_EXPERTS, N_DIM), dtype=jnp.float32) * SCALE
        up_embed = jax.random.normal(k4, (NUM_EXPERTS, N_DIM), dtype=jnp.float32) * SCALE
        return {'x': x, 'W_q': W_q, 'keys': keys, 'down_embed': down_embed, 'up_embed': up_embed}
    _L0_ffn_all = _L0_ffn_setup()
    _L0_ffn_in = {k: v for k, v in _L0_ffn_all.items() if k in ('W_q', 'keys', 'down_embed', 'up_embed')}
    del _L0_ffn_all

    def _L1_attn_setup():
        import jax, jax.numpy as jnp
        import numpy as np

        def _init_linear(key, out_dim, in_dim):
            kw, kb = jax.random.split(key)
            bound = 1.0 / np.sqrt(in_dim)
            W = jax.random.uniform(kw, (out_dim, in_dim), jnp.float32, -bound, bound)
            b = jax.random.uniform(kb, (out_dim,), jnp.float32, -bound, bound)
            return (W, b)
        key = jax.random.key(seed)
        ks = jax.random.split(key, 5)
        B, N, D = (8, 512, 128)
        H, DK = (512, 128)
        x = jax.random.normal(ks[0], (B, N, D), jnp.float32)
        We1, be1 = _init_linear(ks[1], H, D)
        We2, be2 = _init_linear(ks[2], D, H)
        Wk1, bk1 = _init_linear(ks[3], H, D)
        Wk2, bk2 = _init_linear(ks[4], 2 * DK, H)
        return {'x': x, 'We1': We1, 'be1': be1, 'We2': We2, 'be2': be2, 'Wk1': Wk1, 'bk1': bk1, 'Wk2': Wk2, 'bk2': bk2}
    _L1_attn_all = _L1_attn_setup()
    _L1_attn_in = {k: v for k, v in _L1_attn_all.items() if k in ('We1', 'be1', 'We2', 'be2', 'Wk1', 'bk1', 'Wk2', 'bk2')}
    del _L1_attn_all

    def _L1_ffn_setup():
        import jax, jax.numpy as jnp
        import numpy as np
        B, S, H, E, K = (8, 1024, 128, 8, 2)
        key = jax.random.key(seed)
        ks = jax.random.split(key, 7)
        s_h = 1.0 / np.sqrt(H)
        s_2h = 1.0 / np.sqrt(2 * H)
        return {'x': jax.random.normal(ks[0], (B, S, H), dtype=jnp.float32), 'gate_w': jax.random.uniform(ks[1], (H, E), minval=-s_h, maxval=s_h, dtype=jnp.float32), 'gate_b': jax.random.uniform(ks[2], (E,), minval=-s_h, maxval=s_h, dtype=jnp.float32), 'w1': jax.random.uniform(ks[3], (E, H, 2 * H), minval=-s_h, maxval=s_h, dtype=jnp.float32), 'b1': jax.random.uniform(ks[4], (E, 2 * H), minval=-s_h, maxval=s_h, dtype=jnp.float32), 'w2': jax.random.uniform(ks[5], (E, 2 * H, H), minval=-s_2h, maxval=s_2h, dtype=jnp.float32), 'b2': jax.random.uniform(ks[6], (E, H), minval=-s_2h, maxval=s_2h, dtype=jnp.float32)}
    _L1_ffn_all = _L1_ffn_setup()
    _L1_ffn_in = {k: v for k, v in _L1_ffn_all.items() if k in ('gate_w', 'gate_b', 'w1', 'b1', 'w2', 'b2')}
    del _L1_ffn_all
    return {'x': x, 'L0_tok_W': _L0_tok_in['W'], 'L0_tok_b': _L0_tok_in['b'], 'L0_tok_gamma': _L0_tok_in['gamma'], 'L0_tok_beta': _L0_tok_in['beta'], 'L0_attn_proxy': _L0_attn_in['proxy'], 'L0_ffn_W_q': _L0_ffn_in['W_q'], 'L0_ffn_keys': _L0_ffn_in['keys'], 'L0_ffn_down_embed': _L0_ffn_in['down_embed'], 'L0_ffn_up_embed': _L0_ffn_in['up_embed'], 'L1_attn_We1': _L1_attn_in['We1'], 'L1_attn_be1': _L1_attn_in['be1'], 'L1_attn_We2': _L1_attn_in['We2'], 'L1_attn_be2': _L1_attn_in['be2'], 'L1_attn_Wk1': _L1_attn_in['Wk1'], 'L1_attn_bk1': _L1_attn_in['bk1'], 'L1_attn_Wk2': _L1_attn_in['Wk2'], 'L1_attn_bk2': _L1_attn_in['bk2'], 'L1_ffn_gate_w': _L1_ffn_in['gate_w'], 'L1_ffn_gate_b': _L1_ffn_in['gate_b'], 'L1_ffn_w1': _L1_ffn_in['w1'], 'L1_ffn_b1': _L1_ffn_in['b1'], 'L1_ffn_w2': _L1_ffn_in['w2'], 'L1_ffn_b2': _L1_ffn_in['b2']}

def reference(x, L0_tok_W, L0_tok_b, L0_tok_gamma, L0_tok_beta, L0_attn_proxy, L0_ffn_W_q, L0_ffn_keys, L0_ffn_down_embed, L0_ffn_up_embed, L1_attn_We1, L1_attn_be1, L1_attn_We2, L1_attn_be2, L1_attn_Wk1, L1_attn_bk1, L1_attn_Wk2, L1_attn_bk2, L1_ffn_gate_w, L1_ffn_gate_b, L1_ffn_w1, L1_ffn_b1, L1_ffn_w2, L1_ffn_b2):
    import jax
    import jax.numpy as jnp

    def _L0_tok_ref(x, W, b, gamma, beta):
        import jax, jax.numpy as jnp
        import numpy as np
        PATCH_LENGTH = 128
        PATCH_STRIDE = 64
        MODEL_DIM = 128
        LN_EPS = 0.001
        B, T, C = x.shape
        num_patches = (T - PATCH_LENGTH) // PATCH_STRIDE + 1
        idx = jnp.arange(num_patches)[:, None] * PATCH_STRIDE + jnp.arange(PATCH_LENGTH)[None, :]
        patches = x[:, idx, :]
        patches = patches.reshape(B, num_patches, PATCH_LENGTH * C)
        proj = jnp.einsum('bpf,fd->bpd', patches, W) + b
        mean = jnp.mean(proj, axis=-1, keepdims=True)
        var = jnp.mean(jnp.square(proj - mean), axis=-1, keepdims=True)
        out = (proj - mean) * jax.lax.rsqrt(var + LN_EPS) * gamma + beta
        return out

    def _L0_attn_ref(x, proxy):
        import jax, jax.numpy as jnp
        import numpy as np
        num_proxies = proxy.shape[0]
        prods = jnp.einsum('pd,bsd->bps', proxy, x)
        y = jnp.cumsum(prods[..., None] * x[:, None, :, :], axis=2)
        w = jax.nn.softmax(prods / jnp.sqrt(jnp.float32(num_proxies)), axis=1)
        out = jnp.einsum('bps,bpsd->bsd', w, y)
        return out

    def _L0_ffn_ref(x, W_q, keys, down_embed, up_embed):
        import jax, jax.numpy as jnp
        import numpy as np
        N_DIM = 128
        HEADS = 8
        NUM_EXPERTS = 16384
        NUM_KEYS = 64
        DIM_KEY = 64
        TOPK = 16
        SCALE = 0.02
        b, n, d = x.shape
        q = (x @ W_q).reshape(b, n, 2, HEADS, DIM_KEY).transpose(2, 0, 1, 3, 4)
        sim = jnp.einsum('pbnhd,hkpd->pbnhk', q, keys)
        sx, ix = jax.lax.top_k(sim[0], TOPK)
        sy, iy = jax.lax.top_k(sim[1], TOPK)
        all_scores = (sx[..., :, None] + sy[..., None, :]).reshape(b, n, HEADS, TOPK * TOPK)
        scores, pk_idx = jax.lax.top_k(all_scores, TOPK)
        w_down = down_embed[pk_idx]
        w_up = up_embed[pk_idx]
        h = jnp.einsum('bnd,bnhkd->bnhk', x, w_down)
        h = jax.nn.gelu(h, approximate=False)
        h = jax.nn.softmax(scores, axis=-1) * h
        return jnp.einsum('bnhk,bnhkd->bnd', h, w_up)

    def _L1_attn_ref(x, We1, be1, We2, be2, Wk1, bk1, Wk2, bk2):
        import jax, jax.numpy as jnp
        import numpy as np

        def _init_linear(key, out_dim, in_dim):
            kw, kb = jax.random.split(key)
            bound = 1.0 / np.sqrt(in_dim)
            W = jax.random.uniform(kw, (out_dim, in_dim), jnp.float32, -bound, bound)
            b = jax.random.uniform(kb, (out_dim,), jnp.float32, -bound, bound)
            return (W, b)
        embs = jnp.einsum('bnh,dh->bnd', jax.nn.relu(jnp.einsum('bnd,hd->bnh', x, We1) + be1), We2) + be2
        kq = jnp.einsum('bnh,kh->bnk', jax.nn.relu(jnp.einsum('bnd,hd->bnh', x, Wk1) + bk1), Wk2) + bk2
        dk = kq.shape[-1] // 2
        K, Q = (kq[..., :dk], kq[..., dk:])
        A = jax.nn.softmax(jnp.einsum('bnk,bmk->bnm', Q, K), axis=-1)
        return jnp.einsum('bnm,bmd->bnd', A, embs)

    def _L1_ffn_ref(x, gate_w, gate_b, w1, b1, w2, b2):
        import jax, jax.numpy as jnp
        import numpy as np
        B, S, H, E, K = (8, 1024, 128, 8, 2)
        logits = jnp.einsum('bsh,he->bse', x, gate_w) + gate_b
        topk_vals, topk_idx = jax.lax.top_k(logits, K)
        topk_weights = jax.nn.softmax(topk_vals, axis=-1)
        mask = jax.nn.one_hot(topk_idx, E, dtype=topk_weights.dtype)
        weights = jnp.einsum('bske,bsk->bse', mask, topk_weights)
        h = jax.nn.relu(jnp.einsum('bsh,ehf->bsef', x, w1) + b1)
        expert_out = jnp.einsum('bsef,efh->bseh', h, w2) + b2
        return jnp.einsum('bseh,bse->bsh', expert_out, weights)
    h = _L0_tok_ref(x, L0_tok_W, L0_tok_b, L0_tok_gamma, L0_tok_beta)
    h = h + _L0_attn_ref(_layernorm(h, axis=-1), L0_attn_proxy)
    h = h + _L0_ffn_ref(_layernorm(h, axis=-1), L0_ffn_W_q, L0_ffn_keys, L0_ffn_down_embed, L0_ffn_up_embed)
    h = h + _L1_attn_ref(_layernorm(h, axis=-1), L1_attn_We1, L1_attn_be1, L1_attn_We2, L1_attn_be2, L1_attn_Wk1, L1_attn_bk1, L1_attn_Wk2, L1_attn_bk2)
    h = h + _L1_ffn_ref(_layernorm(h, axis=-1), L1_ffn_gate_w, L1_ffn_gate_b, L1_ffn_w1, L1_ffn_b1, L1_ffn_w2, L1_ffn_b2)
    return h

_drawn_inputs = setup_inputs


def setup_inputs(seed=0):
    import zlib

    import numpy as np

    out = dict(_drawn_inputs(seed))
    spreads = {'L0_tok_b': (0.0, 0.1), 'L0_tok_gamma': (1.0, 0.2), 'L0_tok_beta': (0.0, 0.1)}
    factors = {'L0_ffn_W_q': 8.0,
     'L0_ffn_keys': 8.0,
     'L0_ffn_down_embed': 8.0,
     'L0_ffn_up_embed': 8.0,
     'L1_attn_We1': 8.0,
     'L1_attn_be1': 8.0,
     'L1_attn_We2': 8.0,
     'L1_attn_be2': 31.031,
     'L1_attn_Wk1': 8.0,
     'L1_attn_bk1': 8.0,
     'L1_attn_Wk2': 8.0,
     'L1_attn_bk2': 8.0,
     'L1_ffn_gate_w': 8.0,
     'L1_ffn_gate_b': 8.0,
     'L1_ffn_w1': 8.0,
     'L1_ffn_b1': 8.0,
     'L1_ffn_w2': 8.0,
     'L1_ffn_b2': 61.324}
    for name, (base, spread) in spreads.items():
        noise = np.random.default_rng([zlib.crc32(name.encode()), seed]).standard_normal(out[name].shape)
        drawn = base * np.exp(spread * noise) if base else spread * noise
        out[name] = jnp.asarray(drawn.astype(out[name].dtype))
    for name, factor in factors.items():
        out[name] = (out[name] * factor).astype(out[name].dtype)
    return out
```

```python
from contextlib import ExitStack

import concourse.bass as bass
from concourse import mybir

F32 = mybir.dt.float32
ALU = mybir.AluOpType
ACT = mybir.ActivationFunctionType
AX = mybir.AxisListType

D = 128
CLIPS, PATCHES = 64, 4
BLOCK = 128
TILES = CLIPS * PATCHES // 128
PROXIES = 16
HEADS, KEYS, DKEY, TOPK = 8, 64, 64, 16
GROUPS, GHEADS = 2, 4
HIDDEN = 512
CH = HIDDEN // 128
EXPERTS, FCH = 8, 2
NORMS = 5
TOK_EPS, LN_EPS = 1e-3, 1e-5
REMOVED = -3.4028234663852886e38
TAKEN = 3.0e38

RECTS = [(i, max(i, 1), TOPK // (i + 1)) for i in (0, 1, 2, 4, 8)]
PAIRS = sum(ni * nj for _, ni, nj in RECTS)

FIRST = dict(x=2 * TILES * 128, w=2 * D)
CONST = dict(ident=128, gamma=D, beta=D, causal=128, proxy=PROXIES)
LATER = dict(clip=128, down=PAIRS, be1=CH, bk1=CH, bk2=2, b1=EXPERTS * FCH, gate=EXPERTS)
ROWS = dict(up=D, b2=D, tok_b=D, be2=D, gate_b=EXPERTS)
KEYW = dict(wq=HEADS * D, keys=HEADS * KEYS)
MLPW = dict(we1=HIDDEN, wk1=HIDDEN, we2=CH * D, wk2=CH * 2 * D)


def columns(pack):
    at, out = 0, {}
    for name, width in pack.items():
        out[name] = slice(at, at + width)
        at += width
    return out, at


def build(nc, first_in, const_in, later_in, rows_in, keyw_in, mlpw_in, w1_in, w2_in, out):
    with ExitStack() as ctx:
        def sb(name, shape):
            return ctx.enter_context(nc.sbuf_tensor(name, shape, F32))

        def bank(name):
            return ctx.enter_context(nc.psum_tensor(name, [128, 512], F32))

        def sem(name):
            return ctx.enter_context(nc.semaphore(name))

        def each(name):
            return [sem(f"{name}{t}") for t in range(TILES)]

        FC, n_first = columns(FIRST)
        CC, n_const = columns(CONST)
        LC, n_later = columns(LATER)
        RC, n_rows = columns(ROWS)
        KC, n_keyw = columns(KEYW)
        MC, n_mlpw = columns(MLPW)
        first = sb("first", [128, n_first])
        const = sb("const", [128, n_const])
        later = sb("later", [128, n_later])
        rows = sb("rows", [PAIRS, n_rows])
        keyw = sb("keyw", [128, n_keyw])
        mlpw = sb("mlpw", [128, n_mlpw])
        w1 = sb("w1", [128, EXPERTS, FCH, 128])
        w2 = sb("w2", [128, EXPERTS, FCH, D])
        patch_t = first[:, FC["x"]].rearrange("f (c t) -> f c t", c=2)
        tok_w = first[:, FC["w"]].rearrange("f (c d) -> f c d", c=2)
        ident, gamma, beta = const[:, CC["ident"]], const[:, CC["gamma"]], const[:, CC["beta"]]
        causal, proxy_t = const[:, CC["causal"]], const[:, CC["proxy"]]
        other_clip = later[:, LC["clip"]]
        be1, bk1, bk2, b1 = (later[:, LC[n]] for n in ("be1", "bk1", "bk2", "b1"))
        wq_t = keyw[:, KC["wq"]].rearrange("c (h f) -> c h f", h=HEADS)
        keys_t = keyw[:, KC["keys"]].rearrange("c (h k) -> c h k", h=HEADS)
        we1_t, wk1_t = mlpw[:, MC["we1"]], mlpw[:, MC["wk1"]]
        we2_t = mlpw[:, MC["we2"]].rearrange("h (c d) -> h c d", c=CH)
        wk2_t = mlpw[:, MC["wk2"]].rearrange("h (c d) -> h c d", c=CH)

        ones = sb("ones", [1, 128])
        eps = sb("eps", [128, 2])
        proxy_q = sb("proxy_q", [128, PROXIES])
        keymat = sb("keymat", [128, HEADS, 2, KEYS])

        stats = sb("stats", [128, TILES, NORMS, 6])
        mv = sb("mv", [128, TILES, NORMS, 2])
        lnvar = sb("lnvar", [128, TILES, NORMS])
        rstd = sb("rstd", [128, TILES, NORMS])
        centred = sb("centred", [128, TILES, D])
        h = sb("h", [128, TILES, 4, D])
        xn = sb("xn", [128, TILES, 4, D])
        xt = sb("xt", [128, TILES, 4, 128])
        negmax = sb("negmax", [128, TILES, 3])
        total = sb("total", [128, TILES, 3])
        inv = sb("inv", [128, TILES, 3])
        mix = sb("mix", [128, TILES, PROXIES])
        prods_t = sb("prods_t", [PROXIES, TILES, 128])
        mix_t = sb("mix_t", [PROXIES, TILES, 128])
        att_t = sb("att_t", [128, TILES, 128])
        scores = sb("scores", [128, TILES, HEADS, 2, KEYS])
        rest = sb("rest", [128, TILES, HEADS, 2, KEYS])
        best = sb("best", [128, TILES, HEADS, 2, TOPK])
        pairs = sb("pairs", [128, TILES, HEADS, PAIRS])
        shifted = sb("shifted", [128, TILES, HEADS, PAIRS])
        expo = sb("expo", [128, TILES, HEADS, PAIRS])
        left8 = sb("left8", [128, TILES, HEADS, PAIRS])
        left16 = sb("left16", [128, TILES, HEADS, PAIRS])
        pair_top = sb("pair_top", [128, TILES, HEADS, TOPK])
        chosen = sb("chosen", [128, TILES, HEADS, PAIRS])
        norm16 = sb("norm16", [128, TILES, HEADS])
        inv16 = sb("inv16", [128, TILES, HEADS])
        weighted = sb("weighted", [128, TILES, HEADS, PAIRS])
        expert_w = sb("expert_w", [128, TILES, PAIRS])
        gelu = sb("gelu", [128, TILES, PAIRS])
        expert_g = sb("expert_g", [128, TILES, PAIRS])
        expert_t = sb("expert_t", [PAIRS, TILES, 128])
        hk = sb("hk", [128, TILES, CH, 128])
        he = sb("he", [128, TILES, CH, 128])
        kq = sb("kq", [128, TILES, 2, 128])
        embs = sb("embs", [128, TILES, D])
        logits = sb("logits", [128, TILES, 128])
        clip_p = sb("clip_p", [128, TILES, 128])
        clip_t = sb("clip_t", [128, TILES, 128])
        gate = sb("gate", [128, TILES, 16])
        gate_top = sb("gate_top", [128, TILES, 8])
        gate_neg = sb("gate_neg", [128, TILES])
        gate_left = sb("gate_left", [128, TILES, 16])
        gate_exp = sb("gate_exp", [128, TILES, EXPERTS])
        gate_w = sb("gate_w", [128, TILES, EXPERTS])
        gate_t = sb("gate_t", [EXPERTS, TILES, 128])
        hid = sb("hid", [128, TILES, EXPERTS, FCH, 128])
        acc = sb("acc", [128, TILES, EXPERTS + 1, D])
        y = sb("y", [128, TILES, D])

        chain = [bank(f"chain{t}") for t in range(TILES)]
        wide = [bank(f"wide{i}") for i in range(6)]

        first_in_s, const_s, later_s, rows_s, keyw_s, mlpw_s, w1_s, w2_s, stored = (
            sem(n) for n in ("first_in", "const_in", "later_in", "rows_in", "keyw_in", "mlpw_in",
                             "w1_in", "w2_in", "stored"))
        consts_set, proxy_q_ready = sem("consts_set"), sem("proxy_q_ready")
        keymat_done, keymat_ready = sem("keymat_done"), sem("keymat_ready")
        stats_ready, var_ready, lnvar_ready, rstd_ready, h_ready, xn_ready, xt_done, xt_ready = (
            each(n) for n in ("stats_ready", "var_ready", "lnvar_ready", "rstd_ready", "h_ready",
                              "xn_ready", "xt_done", "xt_ready"))
        proj_done, centred_ready = sem("proj_done"), sem("centred_ready")
        (prods_done, prod_max, prods_t_ready, mix_ready, mix_inv, mix_t_done, mix_t_ready, att_done,
         att_ready, att_out) = (sem(n) for n in (
            "prods_done", "prod_max", "prods_t_ready", "mix_ready", "mix_inv", "mix_t_done",
            "mix_t_ready", "att_done", "att_ready", "att_out"))
        (scores_done, down_done, scores_ready, gelu_ready, best8, rest_ready, best16, pairs_ready,
         shifted_ready, expo_ready, pair8, left8_ready, pair16, left16_ready, chosen_ready,
         norm16_ready, inv16_ready, weighted_ready, expert_w_ready, expert_g_ready, expert_t_done,
         expert_t_ready, up_done) = (sem(n) for n in (
            "scores_done", "down_done", "scores_ready", "gelu_ready", "best8", "rest_ready",
            "best16", "pairs_ready", "shifted_ready", "expo_ready", "pair8", "left8_ready",
            "pair16", "left16_ready", "chosen_ready", "norm16_ready", "inv16_ready",
            "weighted_ready", "expert_w_ready", "expert_g_ready", "expert_t_done",
            "expert_t_ready", "up_done"))
        (hk_done, he_done, hk_ready, he_ready, key_done, query_done, embs_done, key_ready,
         query_ready, embs_ready, logits_done, logits_ready, logit_max, clip_ready, clip_inv,
         clip_t_done, clip_t_ready, clip_out) = (sem(n) for n in (
            "hk_done", "he_done", "hk_ready", "he_ready", "key_done", "query_done", "embs_done",
            "key_ready", "query_ready", "embs_ready", "logits_done", "logits_ready", "logit_max",
            "clip_ready", "clip_inv", "clip_t_done", "clip_t_ready", "clip_out"))
        (gate_done, gate_ready, gate_sorted, gate_two, gate_neg_ready, gate_left_ready,
         gate_exp_ready, gate_w_ready, gate_sum, gate_inv, gate_t_done, gate_t_ready, b2_done,
         hid_done, hid_ready, expert_done, acc_ready, y_ready) = (sem(n) for n in (
            "gate_done", "gate_ready", "gate_sorted", "gate_two", "gate_neg_ready",
            "gate_left_ready", "gate_exp_ready", "gate_w_ready", "gate_sum", "gate_inv",
            "gate_t_done", "gate_t_ready", "b2_done", "hid_done", "hid_ready", "expert_done",
            "acc_ready", "y_ready"))

        score_bank = [[wide[0], wide[1]], [wide[2], wide[3]]]
        fold_bank = [wide[2], wide[3]]
        down_bank = [wide[4], wide[5]]
        hk_bank, he_bank, key_bank, query_bank, embs_bank = wide[0], wide[1], wide[2], wide[3], wide[4]
        hid_bank = [wide[0], wide[1], wide[2]]
        expert_bank = [wide[3], wide[4]]
        gate_bank = wide[5]

        block = ctx.enter_context(nc.Block())

        @block.sync
        def _(sp):
            sp.dma_start(first[:, :], first_in).then_inc(first_in_s, 16)
            sp.dma_start(rows[:, :], rows_in).then_inc(rows_s, 16)
            sp.dma_start(later[:, :], later_in).then_inc(later_s, 16)
            sp.dma_start(w1[:, :, :, :], w1_in).then_inc(w1_s, 16)
            for t in range(TILES):
                sp.wait_ge(y_ready, t + 1)
                sp.dma_start(out[t * 128:(t + 1) * 128, :], y[:, t, :]).then_inc(stored, 16)
            sp.wait_ge(stored, 16 * TILES)

        @block.gpsimd
        def _(pool):
            pool.memset(ones[:, :], 1.0).then_inc(consts_set, 1)
            pool.memset(eps[:, 0:1], TOK_EPS).then_inc(consts_set, 1)
            pool.memset(eps[:, 1:2], LN_EPS).then_inc(consts_set, 1)
            for t in range(TILES):
                pool.memset(gate[:, t, EXPERTS:16], REMOVED).then_inc(consts_set, 1)

            def build_pairs(t, g):
                hs = slice(g * GHEADS, (g + 1) * GHEADS)
                pool.wait_ge(best16, 2 * HEADS * t + 2 * GHEADS * (g + 1))
                at = 0
                for i0, ni, nj in RECTS:
                    shape = [128, GHEADS, ni, nj]
                    sum_ = pool.tensor_tensor(
                        pairs[:, t, hs, at:at + ni * nj].rearrange("p h (i j) -> p h i j", j=nj),
                        best[:, t, hs, 0, i0:i0 + ni].unsqueeze(3).to_broadcast(shape),
                        best[:, t, hs, 1, 0:nj].unsqueeze(2).to_broadcast(shape), ALU.add)
                    sum_.then_inc(pairs_ready, 1)
                    at += ni * nj
                pool.wait_ge(pairs_ready, GROUPS * len(RECTS) * t + len(RECTS) * (g + 1))
                pool.tensor_tensor(
                    shifted[:, t, hs, :], pairs[:, t, hs, :],
                    pairs[:, t, hs, 0:1].to_broadcast([128, GHEADS, PAIRS]),
                    ALU.subtract).then_inc(shifted_ready, 1)

            for t in range(TILES):
                for g in range(GROUPS):
                    build_pairs(t, g)

        @block.tensor
        def _(pe):
            def project(t):
                if t == 0:
                    pe.wait_ge(consts_set, 1)
                    pe.wait_ge(rows_s, 16)
                    pe.wait_ge(first_in_s, 16)
                nc.tensor.matmul(chain[t][:, 0:D], ones[0:1, :], rows[0:1, RC["tok_b"]],
                                 start=True, stop=False)
                for c in range(2):
                    last = nc.tensor.matmul(chain[t][:, 0:D], patch_t[:, c, t * 128:(t + 1) * 128],
                                            tok_w[:, c, :], start=False, stop=(c == 1))
                last.then_inc(proj_done, 1)

            def fold_keys():
                pe.wait_ge(keyw_s, 16)
                for p in range(2):
                    lanes = slice(p * DKEY, (p + 1) * DKEY)
                    for hd in range(HEADS):
                        last = nc.tensor.matmul(fold_bank[p][:, hd * KEYS:(hd + 1) * KEYS],
                                                wq_t[lanes, hd, :], keys_t[lanes, hd, :],
                                                start=True, stop=True)
                    last.then_inc(keymat_done, 1)

            def turn_x(t, n):
                pe.wait_ge(xn_ready[t], n + 1)
                nc.tensor.transpose(chain[t][:, 128:256], xn[:, t, n, :], ident)\
                    .then_inc(xt_done[t], 1)

            def proxy_products(t):
                pe.wait_ge(xt_ready[t], 1)
                if t == 0:
                    pe.wait_ge(proxy_q_ready, 1)
                nc.tensor.matmul(chain[t][:, 256:256 + PROXIES], xt[:, t, 0, :], proxy_q[:, :],
                                 start=True, stop=True)
                nc.tensor.matmul(chain[t][0:PROXIES, 384:512], proxy_t, xt[:, t, 0, :],
                                 start=True, stop=True).then_inc(prods_done, 1)

            def turn_mix(t):
                pe.wait_ge(mix_ready, t + 1)
                nc.tensor.transpose(chain[t][0:PROXIES, 0:128], mix[:, t, :], ident)\
                    .then_inc(mix_t_done, 1)

            def proxy_attention(t):
                pe.wait_ge(prods_t_ready, t + 1)
                pe.wait_ge(mix_t_ready, t + 1)
                nc.tensor.matmul(chain[t][:, 128:256], prods_t[:, t, :], mix_t[:, t, :],
                                 start=True, stop=True).then_inc(att_done, 1)

            def proxy_output(t):
                pe.wait_ge(att_ready, t + 1)
                nc.tensor.matmul(chain[t][:, 256:384], att_t[:, t, :], xn[:, t, 0, :],
                                 start=True, stop=True).then_inc(att_out, 1)

            def key_scores(t):
                pe.wait_ge(xt_ready[t], 2)
                if t == 0:
                    pe.wait_ge(keymat_ready, 2)
                for b in range(2):
                    nc.tensor.matmul(
                        score_bank[t][b][:, :], xt[:, t, 1, :],
                        keymat[:, b * GHEADS:(b + 1) * GHEADS, :, :].rearrange("f h a k -> f (h a k)"),
                        start=True, stop=True).then_inc(scores_done, 1)
                if t == 0:
                    pe.wait_ge(later_s, 16)
                nc.tensor.matmul(down_bank[t][:, 0:PAIRS], xt[:, t, 1, :], later[:, LC["down"]],
                                 start=True, stop=True).then_inc(down_done, 1)

            def turn_experts(t):
                pe.wait_ge(expert_g_ready, t + 1)
                nc.tensor.transpose(chain[t][0:PAIRS, 0:128], expert_g[:, t, :], ident)\
                    .then_inc(expert_t_done, 1)

            def expert_up(t):
                pe.wait_ge(expert_t_ready, t + 1)
                nc.tensor.matmul(chain[t][:, 256:384], expert_t[:, t, :], rows[0:PAIRS, RC["up"]],
                                 start=True, stop=True).then_inc(up_done, 1)

            def mlp_hidden(t):
                pe.wait_ge(xt_ready[t], 3)
                if t == 0:
                    pe.wait_ge(mlpw_s, 16)
                    pe.wait_ge(gelu_ready, TILES)
                if t == 1:
                    pe.wait_ge(hid_ready, EXPERTS * FCH)
                    pe.wait_ge(acc_ready, EXPERTS + 1)
                for w, to, done in ((wk1_t, hk_bank, hk_done), (we1_t, he_bank, he_done)):
                    for c in range(CH):
                        last = nc.tensor.matmul(to[:, c * 128:(c + 1) * 128],
                                                w[:, c * 128:(c + 1) * 128], xt[:, t, 2, :],
                                                start=True, stop=True)
                    last.then_inc(done, 1)

            def mlp_outputs(t):
                pe.wait_ge(hk_ready, CH * t + CH)
                for half, to, done in ((0, key_bank, key_done), (1, query_bank, query_done)):
                    for c in range(CH):
                        last = nc.tensor.matmul(to[:, 0:128], wk2_t[:, c, half * D:(half + 1) * D],
                                                hk[:, t, c, :], start=(c == 0), stop=(c == CH - 1))
                    last.then_inc(done, 1)
                nc.tensor.matmul(embs_bank[:, 0:D], ones[0:1, :], rows[0:1, RC["be2"]],
                                 start=True, stop=False)
                pe.wait_ge(he_ready, CH * t + CH)
                for c in range(CH):
                    last = nc.tensor.matmul(embs_bank[:, 0:D], he[:, t, c, :], we2_t[:, c, :],
                                            start=False, stop=(c == CH - 1))
                last.then_inc(embs_done, 1)

            def clip_logits(t):
                pe.wait_ge(key_ready, t + 1)
                pe.wait_ge(query_ready, t + 1)
                nc.tensor.matmul(chain[t][:, 0:128], kq[:, t, 1, :], kq[:, t, 0, :],
                                 start=True, stop=True).then_inc(logits_done, 1)

            def turn_clip(t):
                pe.wait_ge(clip_ready, t + 1)
                nc.tensor.transpose(chain[t][:, 128:256], clip_p[:, t, :], ident)\
                    .then_inc(clip_t_done, 1)

            def clip_output(t):
                pe.wait_ge(clip_t_ready, t + 1)
                pe.wait_ge(embs_ready, t + 1)
                nc.tensor.matmul(chain[t][:, 256:384], clip_t[:, t, :], embs[:, t, :],
                                 start=True, stop=True).then_inc(clip_out, 1)

            def gate_logits(t):
                pe.wait_ge(xt_ready[t], 4)
                nc.tensor.matmul(gate_bank[:, 0:EXPERTS], ones[0:1, :], rows[0:1, RC["gate_b"]],
                                 start=True, stop=False)
                nc.tensor.matmul(gate_bank[:, 0:EXPERTS], xt[:, t, 3, :], later[:, LC["gate"]],
                                 start=False, stop=True).then_inc(gate_done, 1)

            def expert_hidden(t, e):
                if e >= len(hid_bank):
                    pe.wait_ge(hid_ready, EXPERTS * FCH * t + FCH * (e - len(hid_bank) + 1))
                for f in range(FCH):
                    last = nc.tensor.matmul(hid_bank[e % 3][:, f * 128:(f + 1) * 128],
                                            w1[:, e, f, :], xt[:, t, 3, :], start=True, stop=True)
                last.then_inc(hid_done, 1)

            def expert_output(t, e):
                pe.wait_ge(hid_ready, EXPERTS * FCH * t + FCH * (e + 1))
                if e >= 2:
                    pe.wait_ge(acc_ready, (EXPERTS + 1) * t + e)
                for f in range(FCH):
                    last = nc.tensor.matmul(expert_bank[e % 2][:, 0:D], hid[:, t, e, f, :],
                                            w2[:, e, f, :], start=(f == 0), stop=(f == FCH - 1))
                last.then_inc(expert_done, 1)

            def gate_bias(t):
                pe.wait_ge(gate_w_ready, t + 1)
                nc.tensor.transpose(chain[t][0:EXPERTS, 0:128], gate_w[:, t, :], ident)\
                    .then_inc(gate_t_done, 1)
                pe.wait_ge(gate_t_ready, t + 1)
                nc.tensor.matmul(chain[t][:, 384:512], gate_t[:, t, :], rows[0:EXPERTS, RC["b2"]],
                                 start=True, stop=True).then_inc(b2_done, 1)

            def experts(t):
                gate_logits(t)
                if t == 0:
                    pe.wait_ge(w1_s, 16)
                    pe.wait_ge(w2_s, 16)
                expert_hidden(t, 0)
                expert_hidden(t, 1)
                expert_hidden(t, 2)
                gate_bias(t)
                for e in range(EXPERTS):
                    expert_output(t, e)
                    if e + 3 < EXPERTS:
                        expert_hidden(t, e + 3)

            for t in range(TILES):
                project(t)
            pe.wait_ge(const_s, 16)
            fold_keys()
            for t in range(TILES):
                turn_x(t, 0)
            for t in range(TILES):
                proxy_products(t)
            for t in range(TILES):
                turn_mix(t)
            for t in range(TILES):
                proxy_attention(t)
            for t in range(TILES):
                proxy_output(t)
            for t in range(TILES):
                turn_x(t, 1)
                key_scores(t)
            for t in range(TILES):
                turn_experts(t)
                expert_up(t)
                turn_x(t, 2)
                mlp_hidden(t)
                mlp_outputs(t)
                clip_logits(t)
                turn_clip(t)
                clip_output(t)
                turn_x(t, 3)
                experts(t)

        @block.scalar
        def _(act):
            act.dma_start(const[:, :], const_in).then_inc(const_s, 16)
            act.dma_start(keyw[:, :], keyw_in).then_inc(keyw_s, 16)
            act.dma_start(mlpw[:, :], mlpw_in).then_inc(mlpw_s, 16)
            act.dma_start(w2[:, :, :, :], w2_in).then_inc(w2_s, 16)
            nc.scalar.preload_act_table_set("natural_log_exp_and_others")

            def inverse_std(t, n):
                act.wait_ge(var_ready[t], n + 1)
                e = 0 if n == 0 else 1
                nc.scalar.activation(lnvar[:, t, n:n + 1], mv[:, t, n, 1:2], ACT.Ln,
                                     bias=eps[:, e:e + 1]).then_inc(lnvar_ready[t], 1)
                act.wait_ge(lnvar_ready[t], n + 1)
                nc.scalar.activation(rstd[:, t, n:n + 1], lnvar[:, t, n:n + 1], ACT.Exp,
                                     scale=-0.5).then_inc(rstd_ready[t], 1)

            def keep_xt(t, n):
                act.wait_ge(xt_done[t], n + 1)
                nc.scalar.activation(xt[:, t, n, :], chain[t][:, 128:256], ACT.Copy)\
                    .then_inc(xt_ready[t], 1)

            def proxy_softmax(t):
                act.wait_ge(prod_max, t + 1)
                act.wait_ge(prods_t_ready, t + 1)
                nc.scalar.activation(mix[:, t, :], chain[t][:, 256:256 + PROXIES], ACT.Exp,
                                     bias=negmax[:, t, 0:1], accum_out=total[:, t, 0:1])\
                    .then_inc(mix_ready, 1)

            def keep_scores(t, b):
                act.wait_ge(scores_done, 2 * t + b + 1)
                for q in range(2):
                    hs = b * GHEADS + 2 * q
                    nc.scalar.activation(
                        scores[:, t, hs:hs + 2, :, :].rearrange("p h a k -> p (h a k)"),
                        score_bank[t][b][:, q * 256:(q + 1) * 256], ACT.Copy)\
                        .then_inc(scores_ready, 1)

            def expert_gelu(t):
                act.wait_ge(down_done, t + 1)
                nc.scalar.activation(gelu[:, t, :], down_bank[t][:, 0:PAIRS], ACT.Gelu)\
                    .then_inc(gelu_ready, 1)

            def pair_exp(t, g):
                act.wait_ge(shifted_ready, GROUPS * t + g + 1)
                hs = slice(g * GHEADS, (g + 1) * GHEADS)
                nc.scalar.activation(expo[:, t, hs, :], shifted[:, t, hs, :], ACT.Exp)\
                    .then_inc(expo_ready, 1)

            def keep_expert_t(t):
                act.wait_ge(expert_t_done, t + 1)
                nc.scalar.activation(expert_t[:, t, :], chain[t][0:PAIRS, 0:128], ACT.Copy)\
                    .then_inc(expert_t_ready, 1)

            def mlp_relu(t, name):
                to, done, ready, src, bias = {
                    "k": (hk, hk_done, hk_ready, hk_bank, bk1),
                    "e": (he, he_done, he_ready, he_bank, be1)}[name]
                act.wait_ge(done, t + 1)
                for c in range(CH):
                    nc.scalar.activation(to[:, t, c, :], src[:, c * 128:(c + 1) * 128], ACT.Relu,
                                         bias=bias[:, c:c + 1]).then_inc(ready, 1)

            def keep_keys(t):
                act.wait_ge(key_done, t + 1)
                nc.scalar.activation(kq[:, t, 0, :], key_bank[:, 0:128], ACT.Identity,
                                     bias=bk2[:, 0:1]).then_inc(key_ready, 1)
                act.wait_ge(query_done, t + 1)
                nc.scalar.activation(kq[:, t, 1, :], query_bank[:, 0:128], ACT.Identity,
                                     bias=bk2[:, 1:2]).then_inc(query_ready, 1)

            def keep_embs(t):
                act.wait_ge(embs_done, t + 1)
                nc.scalar.activation(embs[:, t, :], embs_bank[:, 0:D], ACT.Copy)\
                    .then_inc(embs_ready, 1)

            def clip_softmax(t):
                act.wait_ge(logit_max, t + 1)
                nc.scalar.activation(clip_p[:, t, :], logits[:, t, :], ACT.Exp,
                                     bias=negmax[:, t, 1:2], accum_out=total[:, t, 1:2])\
                    .then_inc(clip_ready, 1)

            def keep_clip_t(t):
                act.wait_ge(clip_t_done, t + 1)
                nc.scalar.activation(clip_t[:, t, :], chain[t][:, 128:256], ACT.Copy)\
                    .then_inc(clip_t_ready, 1)

            def gate_softmax(t):
                act.wait_ge(gate_neg_ready, t + 1)
                nc.scalar.activation(gate_exp[:, t, :], gate[:, t, 0:EXPERTS], ACT.Exp,
                                     bias=gate_neg[:, t:t + 1]).then_inc(gate_exp_ready, 1)

            def keep_gate_t(t):
                act.wait_ge(gate_t_done, t + 1)
                nc.scalar.activation(gate_t[:, t, :], chain[t][0:EXPERTS, 0:128], ACT.Copy)\
                    .then_inc(gate_t_ready, 1)

            def expert_relu(t, e):
                act.wait_ge(hid_done, EXPERTS * t + e + 1)
                for f in range(FCH):
                    nc.scalar.activation(
                        hid[:, t, e, f, :], hid_bank[e % 3][:, f * 128:(f + 1) * 128], ACT.Relu,
                        bias=b1[:, e * FCH + f:e * FCH + f + 1]).then_inc(hid_ready, 1)

            act.wait_ge(const_s, 16)
            nc.scalar.activation(proxy_q[:, :], proxy_t, ACT.Copy, scale=PROXIES ** -0.5)\
                .then_inc(proxy_q_ready, 1)
            act.wait_ge(consts_set, 3)
            for t in range(TILES):
                inverse_std(t, 0)
            for t in range(TILES):
                inverse_std(t, 1)
            for t in range(TILES):
                keep_xt(t, 0)
            for t in range(TILES):
                proxy_softmax(t)
            for p in range(2):
                act.wait_ge(keymat_done, p + 1)
                nc.scalar.activation(keymat[:, :, p, :],
                                     fold_bank[p][:, :].rearrange("f (h k) -> f h k", h=HEADS),
                                     ACT.Copy).then_inc(keymat_ready, 1)
            for t in range(TILES):
                inverse_std(t, 2)
            for t in range(TILES):
                keep_xt(t, 1)
                keep_scores(t, 0)
                keep_scores(t, 1)
            for t in range(TILES):
                expert_gelu(t)
            nc.scalar.preload_act_table_set("natural_log_exp_and_others")
            act.wait_ge(later_s, 16)
            pair_exp(0, 0)
            pair_exp(0, 1)
            for t in range(TILES):
                keep_expert_t(t)
                inverse_std(t, 3)
                keep_xt(t, 2)
                mlp_relu(t, "k")
                mlp_relu(t, "e")
                keep_keys(t)
                keep_embs(t)
                clip_softmax(t)
                keep_clip_t(t)
                inverse_std(t, 4)
                keep_xt(t, 3)
                if t == 0:
                    pair_exp(1, 0)
                expert_relu(t, 0)
                gate_softmax(t)
                expert_relu(t, 1)
                expert_relu(t, 2)
                if t == 0:
                    pair_exp(1, 1)
                keep_gate_t(t)
                for e in range(3, EXPERTS):
                    expert_relu(t, e)

        @block.vector
        def _(dve):
            def moments(t, n, src):
                nc.vector.bn_stats(stats[:, t, n, :], src).then_inc(stats_ready[t], 1)
                dve.wait_ge(stats_ready[t], n + 1)
                nc.vector.bn_aggr(mv[:, t, n, :], stats[:, t, n, :]).then_inc(var_ready[t], 1)

            def normalize(t, n):
                dve.wait_ge(rstd_ready[t], n + 1)
                nc.vector.tensor_scalar(xn[:, t, n - 1, :], h[:, t, n - 1, :], mv[:, t, n, 0:1],
                                        rstd[:, t, n:n + 1], ALU.subtract, ALU.mult)\
                    .then_inc(xn_ready[t], 1)

            def token_norm(t):
                dve.wait_ge(proj_done, t + 1)
                moments(t, 0, chain[t][:, 0:D])

            def token_centre(t):
                if t == 0:
                    dve.wait_ge(const_s, 16)
                dve.wait_ge(var_ready[t], 1)
                nc.vector.scalar_tensor_tensor(centred[:, t, :], chain[t][:, 0:D], mv[:, t, 0, 0:1],
                                               gamma, ALU.subtract, ALU.mult)\
                    .then_inc(centred_ready, 1)

            def token_out(t):
                dve.wait_ge(centred_ready, t + 1)
                dve.wait_ge(rstd_ready[t], 1)
                nc.vector.scalar_tensor_tensor(h[:, t, 0, :], centred[:, t, :], rstd[:, t, 0:1],
                                               beta, ALU.mult, ALU.add).then_inc(h_ready[t], 1)

            def h_moments(t, n):
                dve.wait_ge(h_ready[t], n)
                moments(t, n, h[:, t, n - 1, :])

            def proxy_max(t):
                dve.wait_ge(prods_done, t + 1)
                nc.vector.tensor_reduce(negmax[:, t, 0:1], chain[t][:, 256:256 + PROXIES],
                                        axis=AX.X, op=ALU.max, negate=True).then_inc(prod_max, 1)
                nc.vector.tensor_copy(prods_t[:, t, :], chain[t][0:PROXIES, 384:512])\
                    .then_inc(prods_t_ready, 1)

            def keep_mix_t(t):
                dve.wait_ge(mix_t_done, t + 1)
                nc.vector.tensor_copy(mix_t[:, t, :], chain[t][0:PROXIES, 0:128])\
                    .then_inc(mix_t_ready, 1)
                nc.vector.reciprocal(inv[:, t, 0:1], total[:, t, 0:1]).then_inc(mix_inv, 1)

            def mask_attention(t):
                dve.wait_ge(att_done, t + 1)
                nc.vector.tensor_tensor(att_t[:, t, :], chain[t][:, 128:256], causal, ALU.mult)\
                    .then_inc(att_ready, 1)

            def add_attention(t):
                dve.wait_ge(att_out, t + 1)
                dve.wait_ge(mix_inv, t + 1)
                nc.vector.scalar_tensor_tensor(h[:, t, 1, :], chain[t][:, 256:384], inv[:, t, 0:1],
                                               h[:, t, 0, :], ALU.mult, ALU.add)\
                    .then_inc(h_ready[t], 1)

            def best_keys(t, hd):
                if hd % 2 == 0:
                    dve.wait_ge(scores_ready, HEADS // 2 * t + hd // 2 + 1)
                for a in range(2):
                    nc.vector.max(best[:, t, hd, a, 0:8], scores[:, t, hd, a, :])\
                        .then_inc(best8, 1)
                for a in range(2):
                    dve.wait_ge(best8, 2 * HEADS * t + 2 * hd + a + 1)
                    nc.vector.match_replace(rest[:, t, hd, a, :], best[:, t, hd, a, 0:8],
                                            scores[:, t, hd, a, :], REMOVED)\
                        .then_inc(rest_ready, 1)
                for a in range(2):
                    dve.wait_ge(rest_ready, 2 * HEADS * t + 2 * hd + a + 1)
                    nc.vector.max(best[:, t, hd, a, 8:16], rest[:, t, hd, a, :])\
                        .then_inc(best16, 1)

            def best_pairs(t, h0):
                two = (h0, h0 + 1)
                dve.wait_ge(pairs_ready, GROUPS * len(RECTS) * t + len(RECTS) * (h0 // GHEADS + 1))
                for hd in two:
                    nc.vector.max(pair_top[:, t, hd, 0:8], pairs[:, t, hd, :]).then_inc(pair8, 1)
                for hd in two:
                    dve.wait_ge(pair8, HEADS * t + hd + 1)
                    nc.vector.match_replace(left8[:, t, hd, :], pair_top[:, t, hd, 0:8],
                                            pairs[:, t, hd, :], REMOVED).then_inc(left8_ready, 1)
                for hd in two:
                    dve.wait_ge(left8_ready, HEADS * t + hd + 1)
                    nc.vector.max(pair_top[:, t, hd, 8:16], left8[:, t, hd, :]).then_inc(pair16, 1)
                for hd in two:
                    dve.wait_ge(pair16, HEADS * t + hd + 1)
                    nc.vector.match_replace(left16[:, t, hd, :], pair_top[:, t, hd, 8:16],
                                            left8[:, t, hd, :], REMOVED).then_inc(left16_ready, 1)

            def pair_weights(t, g):
                hs = slice(g * GHEADS, (g + 1) * GHEADS)
                dve.wait_ge(left16_ready, HEADS * t + GHEADS * (g + 1))
                dve.wait_ge(expo_ready, GROUPS * t + g + 1)
                nc.vector.scalar_tensor_tensor(chosen[:, t, hs, :], left16[:, t, hs, :], REMOVED,
                                               expo[:, t, hs, :], ALU.is_equal, ALU.mult)\
                    .then_inc(chosen_ready, 1)
                dve.wait_ge(chosen_ready, GROUPS * t + g + 1)
                nc.vector.tensor_reduce(norm16[:, t, hs], chosen[:, t, hs, :], axis=AX.X, op=ALU.add)\
                    .then_inc(norm16_ready, 1)
                dve.wait_ge(norm16_ready, GROUPS * t + g + 1)
                nc.vector.reciprocal(inv16[:, t, hs], norm16[:, t, hs]).then_inc(inv16_ready, 1)
                dve.wait_ge(inv16_ready, GROUPS * t + g + 1)
                nc.vector.tensor_tensor(weighted[:, t, hs, :], chosen[:, t, hs, :],
                                        inv16[:, t, hs].unsqueeze(2).to_broadcast([128, GHEADS, PAIRS]),
                                        ALU.mult).then_inc(weighted_ready, 1)

            def expert_weights(t):
                dve.wait_ge(weighted_ready, GROUPS * t + GROUPS)
                nc.vector.tensor_reduce(expert_w[:, t, :],
                                        weighted[:, t, :, :].rearrange("p h c -> p c h"),
                                        axis=AX.X, op=ALU.add).then_inc(expert_w_ready, 1)
                dve.wait_ge(expert_w_ready, t + 1)
                dve.wait_ge(gelu_ready, t + 1)
                nc.vector.tensor_tensor(expert_g[:, t, :], expert_w[:, t, :], gelu[:, t, :],
                                        ALU.mult).then_inc(expert_g_ready, 1)

            def add_experts(t):
                dve.wait_ge(up_done, t + 1)
                nc.vector.tensor_tensor(h[:, t, 2, :], chain[t][:, 256:384], h[:, t, 1, :], ALU.add)\
                    .then_inc(h_ready[t], 1)
                h_moments(t, 3)

            def clip_max(t):
                dve.wait_ge(logits_done, t + 1)
                nc.vector.tensor_tensor(logits[:, t, :], chain[t][:, 0:128], other_clip, ALU.add)\
                    .then_inc(logits_ready, 1)
                dve.wait_ge(logits_ready, t + 1)
                nc.vector.tensor_reduce(negmax[:, t, 1:2], logits[:, t, :], axis=AX.X, op=ALU.max,
                                        negate=True).then_inc(logit_max, 1)

            def add_clip(t):
                dve.wait_ge(clip_ready, t + 1)
                nc.vector.reciprocal(inv[:, t, 1:2], total[:, t, 1:2]).then_inc(clip_inv, 1)
                dve.wait_ge(clip_out, t + 1)
                dve.wait_ge(clip_inv, t + 1)
                nc.vector.scalar_tensor_tensor(h[:, t, 3, :], chain[t][:, 256:384], inv[:, t, 1:2],
                                               h[:, t, 2, :], ALU.mult, ALU.add)\
                    .then_inc(h_ready[t], 1)
                h_moments(t, 4)

            def gate_sort(t):
                dve.wait_ge(gate_done, t + 1)
                nc.vector.tensor_copy(gate[:, t, 0:EXPERTS], gate_bank[:, 0:EXPERTS])\
                    .then_inc(gate_ready, 1)
                dve.wait_ge(gate_ready, t + 1)
                nc.vector.max(gate_top[:, t, :], gate[:, t, :]).then_inc(gate_sorted, 1)
                dve.wait_ge(gate_sorted, t + 1)
                nc.vector.tensor_scalar(gate_neg[:, t:t + 1], gate_top[:, t, 0:1], -1.0, None,
                                        ALU.mult).then_inc(gate_neg_ready, 1)
                nc.vector.memset(gate_top[:, t, 2:8], REMOVED).then_inc(gate_two, 1)

            def gate_weights(t):
                dve.wait_ge(gate_two, t + 1)
                nc.vector.match_replace(gate_left[:, t, :], gate_top[:, t, :], gate[:, t, :], TAKEN)\
                    .then_inc(gate_left_ready, 1)
                dve.wait_ge(gate_left_ready, t + 1)
                dve.wait_ge(gate_exp_ready, t + 1)
                nc.vector.scalar_tensor_tensor(gate_w[:, t, :], gate_left[:, t, 0:EXPERTS], TAKEN,
                                               gate_exp[:, t, :], ALU.is_equal, ALU.mult)\
                    .then_inc(gate_w_ready, 1)
                dve.wait_ge(gate_w_ready, t + 1)
                nc.vector.tensor_reduce(total[:, t, 2:3], gate_w[:, t, :], axis=AX.X, op=ALU.add)\
                    .then_inc(gate_sum, 1)
                dve.wait_ge(gate_sum, t + 1)
                nc.vector.reciprocal(inv[:, t, 2:3], total[:, t, 2:3]).then_inc(gate_inv, 1)

            def start_sum(t):
                dve.wait_ge(b2_done, t + 1)
                nc.vector.tensor_copy(acc[:, t, 0, :], chain[t][:, 384:512]).then_inc(acc_ready, 1)

            def add_expert(t, e):
                dve.wait_ge(expert_done, EXPERTS * t + e + 1)
                dve.wait_ge(acc_ready, (EXPERTS + 1) * t + e + 1)
                nc.vector.scalar_tensor_tensor(acc[:, t, e + 1, :], expert_bank[e % 2][:, 0:D],
                                               gate_w[:, t, e:e + 1], acc[:, t, e, :],
                                               ALU.mult, ALU.add).then_inc(acc_ready, 1)

            def finish(t):
                dve.wait_ge(acc_ready, (EXPERTS + 1) * t + EXPERTS + 1)
                dve.wait_ge(gate_inv, t + 1)
                nc.vector.scalar_tensor_tensor(y[:, t, :], acc[:, t, EXPERTS, :], inv[:, t, 2:3],
                                               h[:, t, 3, :], ALU.mult, ALU.add)\
                    .then_inc(y_ready, 1)

            for t in range(TILES):
                token_norm(t)
            for t in range(TILES):
                token_centre(t)
            for t in range(TILES):
                token_out(t)
                h_moments(t, 1)
            for t in range(TILES):
                normalize(t, 1)
            for t in range(TILES):
                proxy_max(t)
            for t in range(TILES):
                keep_mix_t(t)
            for t in range(TILES):
                mask_attention(t)
            for t in range(TILES):
                add_attention(t)
                h_moments(t, 2)
            for t in range(TILES):
                normalize(t, 2)
            for hd in range(HEADS):
                best_keys(0, hd)
            best_pairs(0, 0)
            best_pairs(0, 2)
            pair_weights(0, 0)
            best_pairs(0, 4)
            best_pairs(0, 6)
            pair_weights(0, 1)
            expert_weights(0)
            best_keys(1, 0)
            add_experts(0)
            best_keys(1, 1)
            normalize(0, 3)
            for hd in range(2, 7):
                best_keys(1, hd)
            clip_max(0)
            best_keys(1, 7)
            best_pairs(1, 0)
            add_clip(0)
            best_pairs(1, 2)
            normalize(0, 4)
            pair_weights(1, 0)
            gate_sort(0)
            best_pairs(1, 4)
            gate_weights(0)
            best_pairs(1, 6)
            start_sum(0)
            add_expert(0, 0)
            add_expert(0, 1)
            pair_weights(1, 1)
            add_expert(0, 2)
            add_expert(0, 3)
            expert_weights(1)
            for e in range(4, EXPERTS):
                add_expert(0, e)
            finish(0)
            add_experts(1)
            normalize(1, 3)
            clip_max(1)
            add_clip(1)
            normalize(1, 4)
            gate_sort(1)
            gate_weights(1)
            start_sum(1)
            for e in range(EXPERTS):
                add_expert(1, e)
            finish(1)


def kernel(**inputs):
    import numpy as np
    import concourse.bacc as bacc
    from concourse.bass_utils import run_bass_kernel_spmd as run

    a = {k: np.asarray(v) for k, v in inputs.items()}

    def pack(layout, parts, height=128):
        where, width = columns(layout)
        out = np.zeros((height, width), np.float32)
        for name, part in parts.items():
            out[:part.shape[0], where[name]] = part
        return out

    def by_column(v):
        return v.reshape(-1, 128).T

    token = np.arange(128)
    same_clip = token[:, None] // PATCHES == token[None, :] // PATCHES
    cells = np.concatenate([(np.arange(i0, i0 + ni)[:, None] * TOPK + np.arange(nj)).ravel()
                            for i0, ni, nj in RECTS])
    x = a["x"].reshape(CLIPS, -1)
    patches = np.stack([x[:, p * BLOCK:(p + 2) * BLOCK] for p in range(PATCHES)], axis=1)
    arrays = {
        "first": pack(FIRST, {
            "x": patches.reshape(-1, 2, 128).transpose(2, 1, 0).reshape(128, -1),
            "w": a["L0_tok_W"].reshape(2, 128, D).transpose(1, 0, 2).reshape(128, -1)}),
        "const": pack(CONST, {
            "ident": np.eye(128, dtype=np.float32),
            "gamma": np.broadcast_to(a["L0_tok_gamma"], (128, D)),
            "beta": np.broadcast_to(a["L0_tok_beta"], (128, D)),
            "causal": (same_clip & (token[:, None] <= token[None, :])).astype(np.float32),
            "proxy": a["L0_attn_proxy"].T}),
        "later": pack(LATER, {
            "clip": np.where(same_clip, 0.0, -1e30).astype(np.float32),
            "down": a["L0_ffn_down_embed"][cells].T,
            "be1": by_column(a["L1_attn_be1"]), "bk1": by_column(a["L1_attn_bk1"]),
            "bk2": by_column(a["L1_attn_bk2"]), "b1": by_column(a["L1_ffn_b1"]),
            "gate": a["L1_ffn_gate_w"]}),
        "rows": pack(ROWS, {
            "up": a["L0_ffn_up_embed"][cells], "b2": a["L1_ffn_b2"],
            "tok_b": a["L0_tok_b"][None], "be2": a["L1_attn_be2"][None],
            "gate_b": a["L1_ffn_gate_b"][None]}, PAIRS),
        "keyw": pack(KEYW, {
            "wq": a["L0_ffn_W_q"].reshape(D, 2, HEADS, DKEY).transpose(1, 3, 2, 0).reshape(128, -1),
            "keys": a["L0_ffn_keys"].transpose(2, 3, 0, 1).reshape(128, -1)}),
        "mlpw": pack(MLPW, {
            "we1": a["L1_attn_We1"].T, "wk1": a["L1_attn_Wk1"].T,
            "we2": a["L1_attn_We2"].T.reshape(CH, 128, D).transpose(1, 0, 2).reshape(128, -1),
            "wk2": a["L1_attn_Wk2"].T.reshape(CH, 128, 2 * D).transpose(1, 0, 2).reshape(128, -1)}),
        "w1": np.ascontiguousarray(a["L1_ffn_w1"].reshape(EXPERTS, D, FCH, 128).transpose(1, 0, 2, 3)),
        "w2": np.ascontiguousarray(a["L1_ffn_w2"].reshape(EXPERTS, FCH, 128, D).transpose(2, 0, 1, 3)),
    }
    nc = bacc.Bacc("TRN2", target_bir_lowering=False, num_devices=1)
    args = [nc.dram_tensor(f"{n}_dram", v.shape, mybir.dt.from_np(v.dtype), kind="ExternalInput").ap()
            for n, v in arrays.items()]
    out = nc.dram_tensor("out_dram", (CLIPS, PATCHES, D), F32, kind="ExternalOutput").ap()
    build(nc, *args, out.rearrange("b p d -> (b p) d"))
    r = run(nc, [{f"{n}_dram": v for n, v in arrays.items()}], core_ids=[0])
    return r.results[0]["out_dram"]
```

```python
from contextlib import ExitStack

import concourse.bass as bass
from concourse import mybir

F32 = mybir.dt.float32
ALU = mybir.AluOpType
ACT = mybir.ActivationFunctionType
AX = mybir.AxisListType

D = 128
CLIPS, PATCHES = 64, 4
BLOCK = 128
TILES = CLIPS * PATCHES // 128
PROXIES = 16
HEADS, KEYS, DKEY, TOPK = 8, 64, 64, 16
GROUPS, GHEADS = 2, 4
WEIGHED = ((0, 4), (4, 6), (6, 8))
HIDDEN = 512
CH = HIDDEN // 128
EXPERTS, FCH = 8, 2
NORMS = 5
TOK_EPS, LN_EPS = 1e-3, 1e-5
REMOVED = -3.4028234663852886e38
TAKEN = 3.0e38

RECTS = [(i, max(i, 1), TOPK // (i + 1)) for i in (0, 1, 2, 4, 8)]
PAIRS = sum(ni * nj for _, ni, nj in RECTS)

FIRST = dict(w=2 * D, tok_b=D)
CONST = dict(ident=128, gamma=D, beta=D, causal=128, proxy=PROXIES)
LATER = dict(clip=128, down=PAIRS, be1=CH, bk1=CH, bk2=2, b1=EXPERTS * FCH, gate=EXPERTS)
ROWS = dict(up=D, b2=D, be2=D, gate_b=EXPERTS)
MLPW = dict(we1=HIDDEN, wk1=HIDDEN, we2=CH * D, wk2=CH * 2 * D)


def columns(pack):
    at, out = 0, {}
    for name, width in pack.items():
        out[name] = slice(at, at + width)
        at += width
    return out, at


def build(nc, patches_in, first_in, const_in, later_in, rows_in, keyw_in, mlpw_in, w1_in, w2_in, out):
    with ExitStack() as ctx:
        def sb(name, shape):
            return ctx.enter_context(nc.sbuf_tensor(name, shape, F32))

        def bank(name):
            return ctx.enter_context(nc.psum_tensor(name, [128, 512], F32))

        def sem(name):
            return ctx.enter_context(nc.semaphore(name))

        def each(name):
            return [sem(f"{name}{t}") for t in range(TILES)]

        FC, n_first = columns(FIRST)
        CC, n_const = columns(CONST)
        LC, n_later = columns(LATER)
        RC, n_rows = columns(ROWS)
        MC, n_mlpw = columns(MLPW)
        first = sb("first", [128, n_first])
        patches = sb("patches", [128, TILES, 2, 128])
        const = sb("const", [128, n_const])
        later = sb("later", [128, n_later])
        rows = sb("rows", [PAIRS, n_rows])
        keyw = sb("keyw", [128, 2, GHEADS, D + 2 * KEYS])
        mlpw = sb("mlpw", [128, n_mlpw])
        w1 = sb("w1", [128, EXPERTS, FCH, 128])
        w2 = sb("w2", [128, EXPERTS, FCH, D])
        tok_w = first[:, FC["w"]].rearrange("f (c d) -> f c d", c=2)
        ident, gamma, beta = const[:, CC["ident"]], const[:, CC["gamma"]], const[:, CC["beta"]]
        causal, proxy_t = const[:, CC["causal"]], const[:, CC["proxy"]]
        other_clip = later[:, LC["clip"]]
        be1, bk1, bk2, b1 = (later[:, LC[n]] for n in ("be1", "bk1", "bk2", "b1"))
        we1_t, wk1_t = mlpw[:, MC["we1"]], mlpw[:, MC["wk1"]]
        we2_t = mlpw[:, MC["we2"]].rearrange("h (c d) -> h c d", c=CH)
        wk2_t = mlpw[:, MC["wk2"]].rearrange("h (c d) -> h c d", c=CH)

        ones = sb("ones", [1, 128])
        eps = sb("eps", [128, 2])
        proxy_q = sb("proxy_q", [128, PROXIES])
        keymat = sb("keymat", [128, HEADS, 2, KEYS])

        stats = sb("stats", [128, TILES, NORMS, 6])
        mv = sb("mv", [128, TILES, NORMS, 2])
        lnvar = sb("lnvar", [128, TILES, NORMS])
        rstd = sb("rstd", [128, TILES, NORMS])
        centred = sb("centred", [128, TILES, D])
        h = sb("h", [128, TILES, 4, D])
        xn = sb("xn", [128, TILES, 4, D])
        xt = sb("xt", [128, TILES, 4, 128])
        negmax = sb("negmax", [128, TILES, 3])
        total = sb("total", [128, TILES, 3])
        inv = sb("inv", [128, TILES, 3])
        mix = sb("mix", [128, TILES, PROXIES])
        prods_t = sb("prods_t", [PROXIES, TILES, 128])
        mix_t = sb("mix_t", [PROXIES, TILES, 128])
        att_t = sb("att_t", [128, TILES, 128])
        scores = sb("scores", [128, TILES, HEADS, 2, KEYS])
        rest = sb("rest", [128, TILES, HEADS, 2, KEYS])
        best = sb("best", [128, TILES, HEADS, 2, TOPK])
        pairs = sb("pairs", [128, TILES, HEADS, PAIRS])
        shifted = sb("shifted", [128, TILES, HEADS, PAIRS])
        expo = sb("expo", [128, TILES, HEADS, PAIRS])
        left8 = sb("left8", [128, TILES, HEADS, PAIRS])
        left16 = sb("left16", [128, TILES, HEADS, PAIRS])
        pair_top = sb("pair_top", [128, TILES, HEADS, TOPK])
        chosen = sb("chosen", [128, TILES, HEADS, PAIRS])
        norm16 = sb("norm16", [128, TILES, HEADS])
        inv16 = sb("inv16", [128, TILES, HEADS])
        scale16 = sb("scale16", [128, TILES, HEADS, 128])
        gelu = sb("gelu", [PAIRS, TILES, 128])
        expert_t = sb("expert_t", [PAIRS, TILES, 128])
        hk = sb("hk", [128, TILES, CH, 128])
        he = sb("he", [128, TILES, CH, 128])
        kq = sb("kq", [128, TILES, 2, 128])
        embs = sb("embs", [128, TILES, D])
        logits = sb("logits", [128, TILES, 128])
        clip_p = sb("clip_p", [128, TILES, 128])
        clip_t = sb("clip_t", [128, TILES, 128])
        gate = sb("gate", [128, TILES, 16])
        gate_top = sb("gate_top", [128, TILES, 8])
        gate_raw = sb("gate_raw", [128, TILES, EXPERTS])
        gate_neg = sb("gate_neg", [128, TILES])
        gate_left = sb("gate_left", [128, TILES, 16])
        gate_exp = sb("gate_exp", [128, TILES, EXPERTS])
        gate_w = sb("gate_w", [128, TILES, EXPERTS])
        gate_t = sb("gate_t", [EXPERTS, TILES, 128])
        hid = sb("hid", [128, TILES, EXPERTS, FCH, 128])
        acc = sb("acc", [128, TILES, EXPERTS + 1, D])
        busy = ctx.enter_context(nc.sbuf_tensor("busy", [128, 256], mybir.dt.bfloat16))

        chain = [bank(f"chain{t}") for t in range(TILES)]
        wide = [bank(f"wide{i}") for i in range(6)]

        patches_s = [sem(f"patches_in{t}") for t in range(TILES)]
        keyw_s = [sem(f"keyw_in{b}") for b in range(2)]
        first_in_s, const_s, later_s, rows_s, mlpw_s, w1_s, w2_s, stored = (
            sem(n) for n in ("first_in", "const_in", "later_in", "rows_in", "mlpw_in",
                             "w1_in", "w2_in", "stored"))
        consts_set, proxy_q_ready, busy_set = sem("consts_set"), sem("proxy_q_ready"), sem("busy_set")
        keymat_done, keymat_ready = sem("keymat_done"), sem("keymat_ready")
        stats_ready, var_ready, lnvar_ready, rstd_ready, h_ready, xn_ready, xt_done, xt_ready = (
            each(n) for n in ("stats_ready", "var_ready", "lnvar_ready", "rstd_ready", "h_ready",
                              "xn_ready", "xt_done", "xt_ready"))
        proj_done, centred_ready = sem("proj_done"), sem("centred_ready")
        (prods_done, prod_max, prods_t_ready, mix_ready, mix_inv, mix_t_done, mix_t_ready, att_done,
         att_ready, att_out) = (sem(n) for n in (
            "prods_done", "prod_max", "prods_t_ready", "mix_ready", "mix_inv", "mix_t_done",
            "mix_t_ready", "att_done", "att_ready", "att_out"))
        (scores_done, down_done, scores_ready, gelu_ready, best8, rest_ready, best16, pairs_ready,
         shifted_ready, expo_ready, pair8, left8_ready, pair16, left16_ready, chosen_ready,
         norm16_ready, inv16_ready, scale16_ready, expert_w_done, expert_t_ready, up_done) = (sem(n) for n in (
            "scores_done", "down_done", "scores_ready", "gelu_ready", "best8", "rest_ready",
            "best16", "pairs_ready", "shifted_ready", "expo_ready", "pair8", "left8_ready",
            "pair16", "left16_ready", "chosen_ready", "norm16_ready", "inv16_ready",
            "scale16_ready", "expert_w_done", "expert_t_ready", "up_done"))
        mlp_done = [sem(f"mlp_done{i}") for i in range(3)]
        mlp_ready = [sem(f"mlp_ready{i}") for i in range(3)]
        (key_done, query_done, embs_done, key_ready,
         query_ready, embs_ready, logits_done, logits_ready, logit_max, clip_ready, clip_inv,
         clip_t_done, clip_t_ready, clip_out) = (sem(n) for n in (
            "key_done", "query_done", "embs_done",
            "key_ready", "query_ready", "embs_ready", "logits_done", "logits_ready", "logit_max",
            "clip_ready", "clip_inv", "clip_t_done", "clip_t_ready", "clip_out"))
        (gate_done, gate_ready, gate_sorted, gate_two, gate_neg_ready, gate_left_ready,
         gate_exp_ready, gate_w_ready, gate_sum, gate_inv, gate_t_done, gate_t_ready, b2_done,
         hid_done, expert_done, gate_raw_ready, b2_ready) = (sem(n) for n in (
            "gate_done", "gate_ready", "gate_sorted", "gate_two", "gate_neg_ready",
            "gate_left_ready", "gate_exp_ready", "gate_w_ready", "gate_sum", "gate_inv",
            "gate_t_done", "gate_t_ready", "b2_done", "hid_done", "expert_done",
            "gate_raw_ready", "b2_ready"))
        hid_ready = [sem(f"hid_ready{f}") for f in range(FCH)]
        acc_ready = each("acc_ready")

        score_bank = [[wide[0], wide[1]], [wide[2], wide[3]]]
        fold_bank = [wide[2], wide[3]]
        down_bank = wide[4]
        mlp_bank = [(wide[4], chain[t], wide[5]) for t in range(TILES)]
        hid_bank = [[wide[0:1] * 2, wide[1:2] * 2], [wide[0:2], wide[4:6]]]
        expert_bank = wide[2:4]

        block = ctx.enter_context(nc.Block())

        @block.sync
        def _(sp):
            sp.dma_start(first[:, :], first_in).then_inc(first_in_s, 16)
            sp.dma_start(patches[:, 1, :, :], patches_in[:, 1, :, :]).then_inc(patches_s[1], 16)
            for b in range(2):
                sp.dma_start(keyw[:, b, :, :], keyw_in[:, b, :, :]).then_inc(keyw_s[b], 16)
            sp.dma_start(later[:, :], later_in).then_inc(later_s, 16)
            sp.dma_start(rows[:, :], rows_in).then_inc(rows_s, 16)
            sp.dma_start(mlpw[:, :], mlpw_in).then_inc(mlpw_s, 16)
            sp.dma_start(w1[:, :, :, :], w1_in).then_inc(w1_s, 16)
            sp.dma_start(w2[:, :, :, :], w2_in).then_inc(w2_s, 16)
            for t in range(TILES):
                sp.wait_ge(acc_ready[t], EXPERTS)
                sp.dma_start(out[t * 128:(t + 1) * 128, :], acc[:, t, EXPERTS, :]).then_inc(stored, 16)
            sp.wait_ge(stored, 16 * TILES)

        @block.gpsimd
        def _(pool):
            pool.memset(ones[:, :], 1.0).then_inc(consts_set, 1)
            pool.memset(eps[:, 0:1], TOK_EPS).then_inc(consts_set, 1)
            pool.memset(eps[:, 1:2], LN_EPS).then_inc(consts_set, 1)
            for t in range(TILES):
                pool.memset(gate[:, t, EXPERTS:16], REMOVED).then_inc(consts_set, 1)

            def build_pairs(t, g):
                hs = slice(g * GHEADS, (g + 1) * GHEADS)
                pool.wait_ge(best16, 2 * HEADS * t + 2 * GHEADS * (g + 1))
                at = 0
                for i0, ni, nj in RECTS:
                    shape = [128, GHEADS, ni, nj]
                    pool.tensor_tensor(
                        pairs[:, t, hs, at:at + ni * nj].rearrange("p h (i j) -> p h i j", j=nj),
                        best[:, t, hs, 0, i0:i0 + ni].unsqueeze(3).to_broadcast(shape),
                        best[:, t, hs, 1, 0:nj].unsqueeze(2).to_broadcast(shape),
                        ALU.add).then_inc(pairs_ready, 1)
                    at += ni * nj
                pool.wait_ge(pairs_ready, len(RECTS) * (GROUPS * t + g + 1))
                pool.tensor_tensor(
                    shifted[:, t, hs, :], pairs[:, t, hs, :],
                    pairs[:, t, hs, 0:1].to_broadcast([128, GHEADS, PAIRS]),
                    ALU.subtract).then_inc(shifted_ready, 1)

            for t in range(TILES):
                for g in range(GROUPS):
                    build_pairs(t, g)

        @block.tensor
        def _(pe):
            def stay_warm(n, bank=wide[5]):
                for _ in range(n):
                    nc.tensor.matmul(bank[:, 0:256], busy[:, 0:128], busy[:, :],
                                     start=True, stop=True)

            def project(t):
                if t == 0:
                    pe.wait_ge(consts_set, 1)
                    pe.wait_ge(first_in_s, 16)
                nc.tensor.matmul(chain[t][:, 0:D], ones[0:1, :], first[0:1, FC["tok_b"]],
                                 start=True, stop=False)
                pe.wait_ge(patches_s[t], 16)
                for c in range(2):
                    last = nc.tensor.matmul(chain[t][:, 0:D], patches[:, t, c, :],
                                            tok_w[:, c, :], start=False, stop=(c == 1))
                last.then_inc(proj_done, 1)

            def fold_keys(h0, n):
                for hd in range(h0, h0 + n):
                    b, g = hd // GHEADS, hd % GHEADS
                    if g == 0:
                        pe.wait_ge(keyw_s[b], 16)
                    nc.tensor.matmul(fold_bank[b][:, g * 2 * KEYS:(g + 1) * 2 * KEYS],
                                     keyw[:, b, g, 0:D], keyw[:, b, g, D:],
                                     start=True, stop=True).then_inc(keymat_done, 1)

            def turn_x(t, n):
                pe.wait_ge(xn_ready[t], n + 1)
                nc.tensor.transpose(chain[t][:, 128:256], xn[:, t, n, :], ident)\
                    .then_inc(xt_done[t], 1)

            def proxy_products(t):
                pe.wait_ge(xt_ready[t], 1)
                if t == 0:
                    pe.wait_ge(proxy_q_ready, 1)
                nc.tensor.matmul(chain[t][:, 256:256 + PROXIES], xt[:, t, 0, :], proxy_q[:, :],
                                 start=True, stop=True)
                nc.tensor.matmul(chain[t][0:PROXIES, 384:512], proxy_t, xt[:, t, 0, :],
                                 start=True, stop=True).then_inc(prods_done, 1)

            def turn_mix(t):
                pe.wait_ge(mix_ready, t + 1)
                nc.tensor.transpose(chain[t][0:PROXIES, 0:128], mix[:, t, :], ident)\
                    .then_inc(mix_t_done, 1)

            def proxy_attention(t):
                pe.wait_ge(prods_t_ready, t + 1)
                pe.wait_ge(mix_t_ready, t + 1)
                nc.tensor.matmul(chain[t][:, 128:256], prods_t[:, t, :], mix_t[:, t, :],
                                 start=True, stop=True).then_inc(att_done, 1)

            def proxy_output(t):
                pe.wait_ge(att_ready, t + 1)
                nc.tensor.matmul(chain[t][:, 256:384], att_t[:, t, :], xn[:, t, 0, :],
                                 start=True, stop=True).then_inc(att_out, 1)

            def key_scores(t):
                pe.wait_ge(xt_ready[t], 2)
                for b in range(2):
                    if t == 0:
                        pe.wait_ge(keymat_ready, b + 1)
                    nc.tensor.matmul(
                        score_bank[t][b][:, :], xt[:, t, 1, :],
                        keymat[:, b * GHEADS:(b + 1) * GHEADS, :, :].rearrange("f h a k -> f (h a k)"),
                        start=True, stop=True).then_inc(scores_done, 1)
                if t == 0:
                    pe.wait_ge(later_s, 16)
                nc.tensor.matmul(down_bank[0:PAIRS, t * 128:(t + 1) * 128], later[:, LC["down"]],
                                 xt[:, t, 1, :], start=True, stop=True).then_inc(down_done, 1)

            def sum_heads(t, h0, h1):
                for hd in range(h0, h1):
                    if hd == h0:
                        pe.wait_ge(chosen_ready, len(WEIGHED) * t + WEIGHED.index((h0, h1)) + 1)
                    pe.wait_ge(scale16_ready, HEADS * t + hd + 1)
                    last = nc.tensor.matmul(chain[t][0:PAIRS, 0:128], chosen[:, t, hd, :],
                                            scale16[:, t, hd, :], start=(hd == 0),
                                            stop=(hd == HEADS - 1))
                if h1 == HEADS:
                    last.then_inc(expert_w_done, 1)

            def expert_up(t):
                pe.wait_ge(expert_t_ready, t + 1)
                if t == 0:
                    pe.wait_ge(rows_s, 16)
                nc.tensor.matmul(chain[t][:, 256:384], expert_t[:, t, :], rows[0:PAIRS, RC["up"]],
                                 start=True, stop=True).then_inc(up_done, 1)

            def mlp_hidden(t):
                pe.wait_ge(xt_ready[t], 3)
                if t == 0:
                    pe.wait_ge(mlpw_s, 16)
                for i in range(3):
                    units = ((0, 1), (2, 3), (0, 1, 2, 3))[i]
                    for c, u in enumerate(units):
                        last = nc.tensor.matmul(mlp_bank[t][i][:, c * 128:(c + 1) * 128],
                                                (wk1_t, we1_t)[i // 2][:, u * 128:(u + 1) * 128],
                                                xt[:, t, 2, :], start=True, stop=True)
                    last.then_inc(mlp_done[i], 1)

            def mlp_outputs(t):
                for half, done in enumerate((key_done, query_done)):
                    for c in range(CH):
                        if c % 2 == 0:
                            pe.wait_ge(mlp_ready[c // 2], 2 * (t + 1))
                        last = nc.tensor.matmul(mlp_bank[t][half][:, 0:128],
                                                wk2_t[:, c, half * D:(half + 1) * D],
                                                hk[:, t, c, :], start=(c == 0), stop=(c == CH - 1))
                    last.then_inc(done, 1)
                pe.wait_ge(mlp_ready[2], CH * (t + 1))
                nc.tensor.matmul(mlp_bank[t][2][:, 0:D], ones[0:1, :], rows[0:1, RC["be2"]],
                                 start=True, stop=False)
                for c in range(CH):
                    last = nc.tensor.matmul(mlp_bank[t][2][:, 0:D], he[:, t, c, :], we2_t[:, c, :],
                                            start=False, stop=(c == CH - 1))
                last.then_inc(embs_done, 1)

            def clip_logits(t):
                pe.wait_ge(key_ready, t + 1)
                pe.wait_ge(query_ready, t + 1)
                nc.tensor.matmul(chain[t][:, 0:128], kq[:, t, 1, :], kq[:, t, 0, :],
                                 start=True, stop=True).then_inc(logits_done, 1)

            def turn_clip(t):
                pe.wait_ge(clip_ready, t + 1)
                nc.tensor.transpose(chain[t][:, 128:256], clip_p[:, t, :], ident)\
                    .then_inc(clip_t_done, 1)

            def clip_output(t):
                pe.wait_ge(clip_t_ready, t + 1)
                pe.wait_ge(embs_ready, t + 1)
                nc.tensor.matmul(chain[t][:, 256:384], clip_t[:, t, :], embs[:, t, :],
                                 start=True, stop=True).then_inc(clip_out, 1)

            def gate_logits(t):
                pe.wait_ge(xt_ready[t], 4)
                nc.tensor.matmul(chain[t][:, 0:EXPERTS], ones[0:1, :], rows[0:1, RC["gate_b"]],
                                 start=True, stop=False)
                nc.tensor.matmul(chain[t][:, 0:EXPERTS], xt[:, t, 3, :], later[:, LC["gate"]],
                                 start=False, stop=True).then_inc(gate_done, 1)

            def expert_hidden(t, e):
                if t == 0 and e == 0:
                    pe.wait_ge(w1_s, 16)
                if e >= 2:
                    for f in range(FCH):
                        pe.wait_ge(hid_ready[f], EXPERTS * t + e - 1)
                for f in range(FCH):
                    nc.tensor.matmul(hid_bank[t][e % 2][f][:, f * 128:(f + 1) * 128],
                                     w1[:, e, f, :], xt[:, t, 3, :],
                                     start=True, stop=True).then_inc(hid_done, 1)

            def expert_output(t, e):
                if t == 0 and e == 0:
                    pe.wait_ge(w2_s, 16)
                if e >= 2:
                    pe.wait_ge(acc_ready[t], e - 1)
                for f in range(FCH):
                    pe.wait_ge(hid_ready[f], EXPERTS * t + e + 1)
                    last = nc.tensor.matmul(expert_bank[e % 2][:, 0:D], hid[:, t, e, f, :],
                                            w2[:, e, f, :], start=(f == 0), stop=(f == FCH - 1))
                last.then_inc(expert_done, 1)

            def turn_gate(t):
                pe.wait_ge(gate_w_ready, t + 1)
                nc.tensor.transpose(chain[t][0:EXPERTS, 0:128], gate_w[:, t, :], ident)\
                    .then_inc(gate_t_done, 1)

            def gate_bias(t):
                pe.wait_ge(gate_t_ready, t + 1)
                nc.tensor.matmul(chain[t][:, 384:512], gate_t[:, t, :], rows[0:EXPERTS, RC["b2"]],
                                 start=True, stop=True).then_inc(b2_done, 1)

            pe.wait_ge(busy_set, 1)
            stay_warm(14)
            project(0)
            stay_warm(2)
            project(1)
            stay_warm(8)
            pe.wait_ge(const_s, 16)
            fold_keys(0, 4)
            turn_x(0, 0)
            stay_warm(3)
            proxy_products(0)
            stay_warm(2)
            turn_x(1, 0)
            stay_warm(2)
            turn_mix(0)
            proxy_products(1)
            stay_warm(1)
            proxy_attention(0)
            stay_warm(5)
            proxy_output(0)
            turn_mix(1)
            fold_keys(4, 2)
            proxy_attention(1)
            fold_keys(6, 2)
            proxy_output(1)
            turn_x(0, 1)
            stay_warm(2)
            key_scores(0)
            turn_x(1, 1)
            stay_warm(2)
            key_scores(1)
            sum_heads(0, *WEIGHED[0])
            pe.wait_ge(gelu_ready, TILES)
            stay_warm(16, wide[3])
            sum_heads(0, *WEIGHED[1])
            stay_warm(2, wide[3])
            sum_heads(0, *WEIGHED[2])
            stay_warm(2, wide[3])
            expert_up(0)
            stay_warm(12, wide[3])
            turn_x(0, 2)
            stay_warm(3, wide[3])
            mlp_hidden(0)
            mlp_outputs(0)
            clip_logits(0)
            stay_warm(8, wide[3])
            turn_clip(0)
            stay_warm(3, wide[3])
            clip_output(0)
            stay_warm(12, wide[3])
            turn_x(0, 3)
            stay_warm(2, wide[3])
            gate_logits(0)
            expert_hidden(0, 0)
            expert_hidden(0, 1)
            expert_output(0, 0)
            expert_hidden(0, 2)
            expert_output(0, 1)
            expert_hidden(0, 3)
            turn_gate(0)
            expert_output(0, 2)
            sum_heads(1, *WEIGHED[0])
            expert_hidden(0, 4)
            gate_bias(0)
            expert_output(0, 3)
            expert_hidden(0, 5)
            sum_heads(1, *WEIGHED[1])
            expert_output(0, 4)
            sum_heads(1, *WEIGHED[2])
            expert_hidden(0, 6)
            expert_up(1)
            expert_output(0, 5)
            expert_hidden(0, 7)
            expert_output(0, 6)
            turn_x(1, 2)
            expert_output(0, 7)
            mlp_hidden(1)
            mlp_outputs(1)
            clip_logits(1)
            pe.wait_ge(acc_ready[0], EXPERTS)
            stay_warm(8, wide[3])
            turn_clip(1)
            stay_warm(3, wide[3])
            clip_output(1)
            stay_warm(12, wide[3])
            turn_x(1, 3)
            stay_warm(2, wide[3])
            gate_logits(1)
            expert_hidden(1, 0)
            for e in range(EXPERTS):
                if e + 1 < EXPERTS:
                    expert_hidden(1, e + 1)
                expert_output(1, e)
                if e == 1:
                    turn_gate(1)
                if e == 2:
                    gate_bias(1)

        @block.scalar
        def _(act):
            act.dma_start(patches[:, 0, :, :], patches_in[:, 0, :, :]).then_inc(patches_s[0], 16)
            act.dma_start(const[:, :], const_in).then_inc(const_s, 16)
            nc.scalar.preload_act_table_set("natural_log_exp_and_others")

            def inverse_std(t, n):
                act.wait_ge(var_ready[t], n + 1)
                e = 0 if n == 0 else 1
                nc.scalar.activation(lnvar[:, t, n:n + 1], mv[:, t, n, 1:2], ACT.Ln,
                                     bias=eps[:, e:e + 1]).then_inc(lnvar_ready[t], 1)
                act.wait_ge(lnvar_ready[t], n + 1)
                nc.scalar.activation(rstd[:, t, n:n + 1], lnvar[:, t, n:n + 1], ACT.Exp,
                                     scale=-0.5).then_inc(rstd_ready[t], 1)

            def keep_xt(t, n):
                act.wait_ge(xt_done[t], n + 1)
                nc.scalar.activation(xt[:, t, n, :], chain[t][:, 128:256], ACT.Copy)\
                    .then_inc(xt_ready[t], 1)

            def proxy_softmax(t):
                act.wait_ge(prod_max, t + 1)
                act.wait_ge(prods_t_ready, t + 1)
                nc.scalar.activation(mix[:, t, :], chain[t][:, 256:256 + PROXIES], ACT.Exp,
                                     bias=negmax[:, t, 0:1], accum_out=total[:, t, 0:1])\
                    .then_inc(mix_ready, 1)

            def keep_keymat(b):
                act.wait_ge(keymat_done, GHEADS * (b + 1))
                nc.scalar.activation(
                    keymat[:, b * GHEADS:(b + 1) * GHEADS, :, :].rearrange("f h a k -> f (h a k)"),
                    fold_bank[b][:, :], ACT.Copy).then_inc(keymat_ready, 1)

            def keep_scores(t, b):
                act.wait_ge(scores_done, 2 * t + b + 1)
                for q in range(2):
                    hs = b * GHEADS + 2 * q
                    nc.scalar.activation(
                        scores[:, t, hs:hs + 2, :, :].rearrange("p h a k -> p (h a k)"),
                        score_bank[t][b][:, q * 256:(q + 1) * 256], ACT.Copy)\
                        .then_inc(scores_ready, 1)

            def expert_gelu(t):
                act.wait_ge(down_done, TILES)
                nc.scalar.activation(gelu[:, t, :], down_bank[0:PAIRS, t * 128:(t + 1) * 128],
                                     ACT.Gelu).then_inc(gelu_ready, 1)

            def pair_exp(t, g):
                act.wait_ge(shifted_ready, GROUPS * t + g + 1)
                hs = slice(g * GHEADS, (g + 1) * GHEADS)
                nc.scalar.activation(expo[:, t, hs, :], shifted[:, t, hs, :], ACT.Exp)\
                    .then_inc(expo_ready, 1)

            def head_scale(t, n):
                h0, h1 = WEIGHED[n]
                act.wait_ge(inv16_ready, len(WEIGHED) * t + n + 1)
                for hd in range(h0, h1):
                    nc.scalar.activation(scale16[:, t, hd, :], ident, ACT.Copy,
                                         scale=inv16[:, t, hd:hd + 1]).then_inc(scale16_ready, 1)

            def mlp_relu(t, i):
                to, bias = ((hk, bk1), (he, be1))[i // 2]
                act.wait_ge(mlp_done[i], t + 1)
                for c, u in enumerate(((0, 1), (2, 3), (0, 1, 2, 3))[i]):
                    nc.scalar.activation(to[:, t, u, :], mlp_bank[t][i][:, c * 128:(c + 1) * 128],
                                         ACT.Relu, bias=bias[:, u:u + 1]).then_inc(mlp_ready[i], 1)

            def keep_keys(t):
                act.wait_ge(key_done, t + 1)
                nc.scalar.activation(kq[:, t, 0, :], mlp_bank[t][0][:, 0:128], ACT.Identity,
                                     bias=bk2[:, 0:1]).then_inc(key_ready, 1)

            def keep_queries(t):
                act.wait_ge(query_done, t + 1)
                nc.scalar.activation(kq[:, t, 1, :], mlp_bank[t][1][:, 0:128], ACT.Identity,
                                     bias=bk2[:, 1:2]).then_inc(query_ready, 1)

            def keep_embs(t):
                act.wait_ge(embs_done, t + 1)
                nc.scalar.activation(embs[:, t, :], mlp_bank[t][2][:, 0:D], ACT.Copy)\
                    .then_inc(embs_ready, 1)

            def clip_softmax(t):
                act.wait_ge(logit_max, t + 1)
                nc.scalar.activation(clip_p[:, t, :], logits[:, t, :], ACT.Exp,
                                     bias=negmax[:, t, 1:2], accum_out=total[:, t, 1:2])\
                    .then_inc(clip_ready, 1)

            def keep_clip_t(t):
                act.wait_ge(clip_t_done, t + 1)
                nc.scalar.activation(clip_t[:, t, :], chain[t][:, 128:256], ACT.Copy)\
                    .then_inc(clip_t_ready, 1)

            def gate_softmax(t):
                act.wait_ge(gate_neg_ready, t + 1)
                nc.scalar.activation(gate_exp[:, t, :], gate[:, t, 0:EXPERTS], ACT.Exp,
                                     bias=gate_neg[:, t:t + 1]).then_inc(gate_exp_ready, 1)

            def keep_gate_t(t):
                act.wait_ge(gate_t_done, t + 1)
                nc.scalar.activation(gate_t[:, t, :], chain[t][0:EXPERTS, 0:128], ACT.Copy)\
                    .then_inc(gate_t_ready, 1)

            def expert_relu(t, e, halves):
                for f in halves:
                    act.wait_ge(hid_done, FCH * (EXPERTS * t + e) + (f + 1 if t else FCH))
                    nc.scalar.activation(
                        hid[:, t, e, f, :], hid_bank[t][e % 2][f][:, f * 128:(f + 1) * 128], ACT.Relu,
                        bias=b1[:, e * FCH + f:e * FCH + f + 1]).then_inc(hid_ready[f], 1)

            act.wait_ge(const_s, 16)
            nc.scalar.activation(proxy_q[:, :], proxy_t, ACT.Copy, scale=PROXIES ** -0.5)\
                .then_inc(proxy_q_ready, 1)
            act.wait_ge(consts_set, 3)
            inverse_std(0, 0)
            inverse_std(0, 1)
            inverse_std(1, 0)
            keep_xt(0, 0)
            keep_keymat(0)
            inverse_std(1, 1)
            proxy_softmax(0)
            keep_xt(1, 0)
            proxy_softmax(1)
            inverse_std(0, 2)
            keep_keymat(1)
            keep_xt(0, 1)
            keep_scores(0, 0)
            keep_scores(0, 1)
            inverse_std(1, 2)
            keep_xt(1, 1)
            keep_scores(1, 0)
            keep_scores(1, 1)
            for t in range(TILES):
                expert_gelu(t)
            nc.scalar.preload_act_table_set("natural_log_exp_and_others")
            act.wait_ge(later_s, 16)
            pair_exp(0, 0)
            pair_exp(0, 1)
            for n in range(len(WEIGHED)):
                head_scale(0, n)
            inverse_std(0, 3)
            keep_xt(0, 2)
            for i in range(3):
                mlp_relu(0, i)
            keep_keys(0)
            keep_queries(0)
            pair_exp(1, 0)
            keep_embs(0)
            clip_softmax(0)
            keep_clip_t(0)
            inverse_std(0, 4)
            keep_xt(0, 3)
            pair_exp(1, 1)
            expert_relu(0, 0, (0, 1))
            gate_softmax(0)
            expert_relu(0, 1, (0, 1))
            head_scale(1, 0)
            expert_relu(0, 2, (0, 1))
            expert_relu(0, 3, (0, 1))
            keep_gate_t(0)
            head_scale(1, 1)
            expert_relu(0, 4, (0, 1))
            head_scale(1, 2)
            expert_relu(0, 5, (0, 1))
            expert_relu(0, 6, (0, 1))
            inverse_std(1, 3)
            expert_relu(0, 7, (0, 1))
            keep_xt(1, 2)
            mlp_relu(1, 0)
            mlp_relu(1, 2)
            keep_keys(1)
            keep_queries(1)
            keep_embs(1)
            clip_softmax(1)
            keep_clip_t(1)
            inverse_std(1, 4)
            keep_xt(1, 3)
            expert_relu(1, 0, (0,))
            expert_relu(1, 1, (0,))
            gate_softmax(1)
            expert_relu(1, 2, (0,))
            expert_relu(1, 3, (0,))
            keep_gate_t(1)
            for e in range(4, EXPERTS):
                expert_relu(1, e, (0,))

        @block.vector
        def _(dve):
            dve.memset(busy[:, :], 1.0).then_inc(busy_set, 1)

            def moments(t, n, src):
                nc.vector.bn_stats(stats[:, t, n, :], src).then_inc(stats_ready[t], 1)
                dve.wait_ge(stats_ready[t], n + 1)
                nc.vector.bn_aggr(mv[:, t, n, :], stats[:, t, n, :]).then_inc(var_ready[t], 1)

            def normalize(t, n):
                dve.wait_ge(rstd_ready[t], n + 1)
                nc.vector.tensor_scalar(xn[:, t, n - 1, :], h[:, t, n - 1, :], mv[:, t, n, 0:1],
                                        rstd[:, t, n:n + 1], ALU.subtract, ALU.mult)\
                    .then_inc(xn_ready[t], 1)

            def token_norm(t):
                dve.wait_ge(proj_done, t + 1)
                moments(t, 0, chain[t][:, 0:D])

            def token_centre(t):
                if t == 0:
                    dve.wait_ge(const_s, 16)
                dve.wait_ge(var_ready[t], 1)
                nc.vector.scalar_tensor_tensor(centred[:, t, :], chain[t][:, 0:D], mv[:, t, 0, 0:1],
                                               gamma, ALU.subtract, ALU.mult)\
                    .then_inc(centred_ready, 1)

            def token_out(t):
                dve.wait_ge(centred_ready, t + 1)
                dve.wait_ge(rstd_ready[t], 1)
                nc.vector.scalar_tensor_tensor(h[:, t, 0, :], centred[:, t, :], rstd[:, t, 0:1],
                                               beta, ALU.mult, ALU.add).then_inc(h_ready[t], 1)

            def h_moments(t, n):
                dve.wait_ge(h_ready[t], n)
                moments(t, n, h[:, t, n - 1, :])

            def proxy_max(t):
                dve.wait_ge(prods_done, t + 1)
                nc.vector.tensor_reduce(negmax[:, t, 0:1], chain[t][:, 256:256 + PROXIES],
                                        axis=AX.X, op=ALU.max, negate=True).then_inc(prod_max, 1)
                nc.vector.tensor_copy(prods_t[:, t, :], chain[t][0:PROXIES, 384:512])\
                    .then_inc(prods_t_ready, 1)

            def keep_mix_t(t):
                dve.wait_ge(mix_t_done, t + 1)
                nc.vector.tensor_copy(mix_t[:, t, :], chain[t][0:PROXIES, 0:128])\
                    .then_inc(mix_t_ready, 1)
                nc.vector.reciprocal(inv[:, t, 0:1], total[:, t, 0:1]).then_inc(mix_inv, 1)

            def mask_attention(t):
                dve.wait_ge(att_done, t + 1)
                nc.vector.tensor_tensor(att_t[:, t, :], chain[t][:, 128:256], causal, ALU.mult)\
                    .then_inc(att_ready, 1)

            def add_attention(t):
                dve.wait_ge(att_out, t + 1)
                dve.wait_ge(mix_inv, t + 1)
                nc.vector.scalar_tensor_tensor(h[:, t, 1, :], chain[t][:, 256:384], inv[:, t, 0:1],
                                               h[:, t, 0, :], ALU.mult, ALU.add)\
                    .then_inc(h_ready[t], 1)

            def best_keys(t, hd):
                if hd % 2 == 0:
                    dve.wait_ge(scores_ready, HEADS // 2 * t + hd // 2 + 1)
                for a in range(2):
                    nc.vector.max(best[:, t, hd, a, 0:8], scores[:, t, hd, a, :]).then_inc(best8, 1)
                for a in range(2):
                    dve.wait_ge(best8, 2 * HEADS * t + 2 * hd + a + 1)
                    nc.vector.match_replace(rest[:, t, hd, a, :], best[:, t, hd, a, 0:8],
                                            scores[:, t, hd, a, :], REMOVED).then_inc(rest_ready, 1)
                for a in range(2):
                    dve.wait_ge(rest_ready, 2 * HEADS * t + 2 * hd + a + 1)
                    nc.vector.max(best[:, t, hd, a, 8:16], rest[:, t, hd, a, :]).then_inc(best16, 1)

            def best_pairs(t, h0):
                two = (h0, h0 + 1)
                dve.wait_ge(pairs_ready, len(RECTS) * (GROUPS * t + h0 // GHEADS + 1))
                for hd in two:
                    nc.vector.max(pair_top[:, t, hd, 0:8], pairs[:, t, hd, :]).then_inc(pair8, 1)
                for hd in two:
                    dve.wait_ge(pair8, HEADS * t + hd + 1)
                    nc.vector.match_replace(left8[:, t, hd, :], pair_top[:, t, hd, 0:8],
                                            pairs[:, t, hd, :], REMOVED).then_inc(left8_ready, 1)
                for hd in two:
                    dve.wait_ge(left8_ready, HEADS * t + hd + 1)
                    nc.vector.max(pair_top[:, t, hd, 8:16], left8[:, t, hd, :]).then_inc(pair16, 1)
                for hd in two:
                    dve.wait_ge(pair16, HEADS * t + hd + 1)
                    nc.vector.match_replace(left16[:, t, hd, :], pair_top[:, t, hd, 8:16],
                                            left8[:, t, hd, :], REMOVED).then_inc(left16_ready, 1)

            def pair_weights(t, n):
                h0, h1 = WEIGHED[n]
                hs, at = slice(h0, h1), len(WEIGHED) * t + n + 1
                dve.wait_ge(left16_ready, HEADS * t + h1)
                dve.wait_ge(expo_ready, GROUPS * t + (h1 - 1) // GHEADS + 1)
                nc.vector.scalar_tensor_tensor(chosen[:, t, hs, :], left16[:, t, hs, :], REMOVED,
                                               expo[:, t, hs, :], ALU.is_equal, ALU.mult)\
                    .then_inc(chosen_ready, 1)
                dve.wait_ge(chosen_ready, at)
                nc.vector.tensor_reduce(norm16[:, t, hs], chosen[:, t, hs, :], axis=AX.X, op=ALU.add)\
                    .then_inc(norm16_ready, 1)
                dve.wait_ge(norm16_ready, at)
                nc.vector.reciprocal(inv16[:, t, hs], norm16[:, t, hs]).then_inc(inv16_ready, 1)

            def expert_mix(t):
                dve.wait_ge(expert_w_done, t + 1)
                if t == 0:
                    dve.wait_ge(gelu_ready, TILES)
                nc.vector.tensor_tensor(expert_t[:, t, :], chain[t][0:PAIRS, 0:128], gelu[:, t, :],
                                        ALU.mult).then_inc(expert_t_ready, 1)

            def add_experts(t):
                dve.wait_ge(up_done, t + 1)
                nc.vector.tensor_tensor(h[:, t, 2, :], chain[t][:, 256:384], h[:, t, 1, :], ALU.add)\
                    .then_inc(h_ready[t], 1)
                h_moments(t, 3)

            def mlp_relu():
                dve.wait_ge(mlp_done[1], 2)
                for c, u in enumerate((2, 3)):
                    nc.vector.tensor_scalar(hk[:, 1, u, :], mlp_bank[1][1][:, c * 128:(c + 1) * 128],
                                            bk1[:, u:u + 1], 0.0, ALU.add, ALU.max)\
                        .then_inc(mlp_ready[1], 1)

            def clip_max(t):
                dve.wait_ge(logits_done, t + 1)
                nc.vector.tensor_tensor(logits[:, t, :], chain[t][:, 0:128], other_clip, ALU.add)\
                    .then_inc(logits_ready, 1)
                dve.wait_ge(logits_ready, t + 1)
                nc.vector.tensor_reduce(negmax[:, t, 1:2], logits[:, t, :], axis=AX.X, op=ALU.max,
                                        negate=True).then_inc(logit_max, 1)

            def add_clip(t):
                dve.wait_ge(clip_ready, t + 1)
                nc.vector.reciprocal(inv[:, t, 1:2], total[:, t, 1:2]).then_inc(clip_inv, 1)
                dve.wait_ge(clip_out, t + 1)
                dve.wait_ge(clip_inv, t + 1)
                nc.vector.scalar_tensor_tensor(h[:, t, 3, :], chain[t][:, 256:384], inv[:, t, 1:2],
                                               h[:, t, 2, :], ALU.mult, ALU.add)\
                    .then_inc(h_ready[t], 1)
                h_moments(t, 4)

            def gate_sort(t):
                dve.wait_ge(gate_done, t + 1)
                nc.vector.tensor_copy(gate[:, t, 0:EXPERTS], chain[t][:, 0:EXPERTS])\
                    .then_inc(gate_ready, 1)
                dve.wait_ge(gate_ready, t + 1)
                nc.vector.max(gate_top[:, t, :], gate[:, t, :]).then_inc(gate_sorted, 1)
                dve.wait_ge(gate_sorted, t + 1)
                nc.vector.tensor_scalar(gate_neg[:, t:t + 1], gate_top[:, t, 0:1], -1.0, None,
                                        ALU.mult).then_inc(gate_neg_ready, 1)
                nc.vector.memset(gate_top[:, t, 2:8], REMOVED).then_inc(gate_two, 1)

            def gate_weights(t):
                dve.wait_ge(gate_two, t + 1)
                nc.vector.match_replace(gate_left[:, t, :], gate_top[:, t, :], gate[:, t, :], TAKEN)\
                    .then_inc(gate_left_ready, 1)
                dve.wait_ge(gate_left_ready, t + 1)
                dve.wait_ge(gate_exp_ready, t + 1)
                nc.vector.scalar_tensor_tensor(gate_raw[:, t, :], gate_left[:, t, 0:EXPERTS], TAKEN,
                                               gate_exp[:, t, :], ALU.is_equal, ALU.mult)\
                    .then_inc(gate_raw_ready, 1)
                dve.wait_ge(gate_raw_ready, t + 1)
                nc.vector.tensor_reduce(total[:, t, 2:3], gate_raw[:, t, :], axis=AX.X, op=ALU.add)\
                    .then_inc(gate_sum, 1)
                dve.wait_ge(gate_sum, t + 1)
                nc.vector.reciprocal(inv[:, t, 2:3], total[:, t, 2:3]).then_inc(gate_inv, 1)
                dve.wait_ge(gate_inv, t + 1)
                nc.vector.tensor_scalar(gate_w[:, t, :], gate_raw[:, t, :], inv[:, t, 2:3], None,
                                        ALU.mult).then_inc(gate_w_ready, 1)

            def expert_relu(e):
                dve.wait_ge(hid_done, FCH * (EXPERTS + e + 1))
                nc.vector.tensor_scalar(hid[:, 1, e, 1, :], hid_bank[1][e % 2][1][:, 128:256],
                                        b1[:, e * FCH + 1:e * FCH + 2], 0.0, ALU.add, ALU.max)\
                    .then_inc(hid_ready[1], 1)

            def add_expert(t, e):
                dve.wait_ge(expert_done, EXPERTS * t + e + 1)
                before = acc[:, t, e, :]
                if e == 0:
                    dve.wait_ge(gate_w_ready, t + 1)
                    before = h[:, t, 3, :]
                elif e == 5:
                    dve.wait_ge(b2_ready, t + 1)
                    before = acc[:, t, 0, :]
                else:
                    dve.wait_ge(acc_ready[t], e)
                nc.vector.scalar_tensor_tensor(acc[:, t, e + 1, :], expert_bank[e % 2][:, 0:D],
                                               gate_w[:, t, e:e + 1], before, ALU.mult, ALU.add)\
                    .then_inc(acc_ready[t], 1)

            def add_biases(t):
                dve.wait_ge(b2_done, t + 1)
                dve.wait_ge(acc_ready[t], 5)
                nc.vector.tensor_tensor(acc[:, t, 0, :], chain[t][:, 384:512], acc[:, t, 5, :],
                                        ALU.add).then_inc(b2_ready, 1)

            token_norm(0)
            token_centre(0)
            token_out(0)
            h_moments(0, 1)
            token_norm(1)
            normalize(0, 1)
            token_centre(1)
            token_out(1)
            h_moments(1, 1)
            proxy_max(0)
            normalize(1, 1)
            keep_mix_t(0)
            proxy_max(1)
            mask_attention(0)
            add_attention(0)
            h_moments(0, 2)
            keep_mix_t(1)
            normalize(0, 2)
            mask_attention(1)
            best_keys(0, 0)
            add_attention(1)
            h_moments(1, 2)
            best_keys(0, 1)
            normalize(1, 2)
            for hd in range(2, HEADS):
                best_keys(0, hd)
            best_pairs(0, 0)
            best_pairs(0, 2)
            pair_weights(0, 0)
            best_pairs(0, 4)
            pair_weights(0, 1)
            best_pairs(0, 6)
            pair_weights(0, 2)
            best_keys(1, 0)
            best_keys(1, 1)
            expert_mix(0)
            best_keys(1, 2)
            add_experts(0)
            best_keys(1, 3)
            normalize(0, 3)
            for hd in range(4, HEADS):
                best_keys(1, hd)
            best_pairs(1, 0)
            best_pairs(1, 2)
            clip_max(0)
            best_pairs(1, 4)
            add_clip(0)
            best_pairs(1, 6)
            normalize(0, 4)
            pair_weights(1, 0)
            gate_sort(0)
            pair_weights(1, 1)
            gate_weights(0)
            pair_weights(1, 2)
            add_expert(0, 0)
            add_expert(0, 1)
            add_expert(0, 2)
            add_expert(0, 3)
            expert_mix(1)
            add_expert(0, 4)
            add_biases(0)
            add_experts(1)
            add_expert(0, 5)
            normalize(1, 3)
            add_expert(0, 6)
            add_expert(0, 7)
            mlp_relu()
            clip_max(1)
            add_clip(1)
            normalize(1, 4)
            gate_sort(1)
            expert_relu(0)
            expert_relu(1)
            gate_weights(1)
            for e in range(EXPERTS):
                if e == 5:
                    add_biases(1)
                add_expert(1, e)
                if e + 2 < EXPERTS:
                    expert_relu(e + 2)


def kernel(**inputs):
    import numpy as np
    import concourse.bacc as bacc
    from concourse.bass_utils import run_bass_kernel_spmd as run

    a = {k: np.asarray(v) for k, v in inputs.items()}

    def pack(layout, parts, height=128):
        where, width = columns(layout)
        out = np.zeros((height, width), np.float32)
        for name, part in parts.items():
            out[:part.shape[0], where[name]] = part
        return out

    def by_column(v):
        return v.reshape(-1, 128).T

    token = np.arange(128)
    same_clip = token[:, None] // PATCHES == token[None, :] // PATCHES
    cells = np.concatenate([(np.arange(i0, i0 + ni)[:, None] * TOPK + np.arange(nj)).ravel()
                            for i0, ni, nj in RECTS])
    keys = np.zeros((2, DKEY, HEADS, 2, KEYS), np.float32)
    for p in range(2):
        keys[p, :, :, p, :] = a["L0_ffn_keys"][:, :, p, :].transpose(2, 0, 1)
    wq = a["L0_ffn_W_q"].reshape(D, 2, HEADS, DKEY).transpose(1, 3, 2, 0)
    x = a["x"].reshape(CLIPS, -1)
    patches = np.stack([x[:, p * BLOCK:(p + 2) * BLOCK] for p in range(PATCHES)], axis=1)
    arrays = {
        "patches": np.ascontiguousarray(
            patches.reshape(TILES, 128, 2, 128).transpose(3, 0, 2, 1)),
        "first": pack(FIRST, {
            "w": a["L0_tok_W"].reshape(2, 128, D).transpose(1, 0, 2).reshape(128, -1),
            "tok_b": a["L0_tok_b"][None]}),
        "const": pack(CONST, {
            "ident": np.eye(128, dtype=np.float32),
            "gamma": np.broadcast_to(a["L0_tok_gamma"], (128, D)),
            "beta": np.broadcast_to(a["L0_tok_beta"], (128, D)),
            "causal": (same_clip & (token[:, None] <= token[None, :])).astype(np.float32),
            "proxy": a["L0_attn_proxy"].T}),
        "later": pack(LATER, {
            "clip": np.where(same_clip, 0.0, -1e30).astype(np.float32),
            "down": a["L0_ffn_down_embed"][cells].T,
            "be1": by_column(a["L1_attn_be1"]), "bk1": by_column(a["L1_attn_bk1"]),
            "bk2": by_column(a["L1_attn_bk2"]), "b1": by_column(a["L1_ffn_b1"]),
            "gate": a["L1_ffn_gate_w"]}),
        "rows": pack(ROWS, {
            "up": a["L0_ffn_up_embed"][cells], "b2": a["L1_ffn_b2"],
            "be2": a["L1_attn_be2"][None],
            "gate_b": a["L1_ffn_gate_b"][None]}, PAIRS),
        "keyw": np.concatenate([wq.reshape(128, HEADS, D), keys.reshape(128, HEADS, 2 * KEYS)], axis=2)
        .reshape(128, 2, GHEADS, D + 2 * KEYS),
        "mlpw": pack(MLPW, {
            "we1": a["L1_attn_We1"].T, "wk1": a["L1_attn_Wk1"].T,
            "we2": a["L1_attn_We2"].T.reshape(CH, 128, D).transpose(1, 0, 2).reshape(128, -1),
            "wk2": a["L1_attn_Wk2"].T.reshape(CH, 128, 2 * D).transpose(1, 0, 2).reshape(128, -1)}),
        "w1": np.ascontiguousarray(a["L1_ffn_w1"].reshape(EXPERTS, D, FCH, 128).transpose(1, 0, 2, 3)),
        "w2": np.ascontiguousarray(a["L1_ffn_w2"].reshape(EXPERTS, FCH, 128, D).transpose(2, 0, 1, 3)),
    }
    nc = bacc.Bacc("TRN2", target_bir_lowering=False, num_devices=1)
    args = [nc.dram_tensor(f"{n}_dram", v.shape, mybir.dt.from_np(v.dtype), kind="ExternalInput").ap()
            for n, v in arrays.items()]
    out = nc.dram_tensor("out_dram", (CLIPS, PATCHES, D), F32, kind="ExternalOutput").ap()
    build(nc, *args, out.rearrange("b p d -> (b p) d"))
    r = run(nc, [{f"{n}_dram": v for n, v in arrays.items()}], core_ids=[0])
    return r.results[0]["out_dram"]
```

```python
from contextlib import ExitStack

import concourse.bass as bass
from concourse import mybir

F32 = mybir.dt.float32
ALU = mybir.AluOpType
ACT = mybir.ActivationFunctionType
AX = mybir.AxisListType

D = 128
CLIPS, PATCHES = 64, 4
BLOCK = 128
TILES = CLIPS * PATCHES // 128
PROXIES = 16
HEADS, KEYS, DKEY, TOPK = 8, 64, 64, 16
GROUPS, GHEADS = 2, 4
SCORED = ((0, 1), (1, 2), (2, 4), (4, 6), (6, 8))
WEIGHED = ((0, 4), (4, 6), (6, 8))
HIDDEN = 512
CH = HIDDEN // 128
EXPERTS, FCH = 8, 2
BIASES_AT = (5, 2)
NORMS = 5
TOK_EPS, LN_EPS = 1e-3, 1e-5
REMOVED = -3.4028234663852886e38
TAKEN = 3.0e38

RECTS = [(i, max(i, 1), TOPK // (i + 1)) for i in (0, 1, 2, 4, 8)]
PAIRS = sum(ni * nj for _, ni, nj in RECTS)

FIRST = dict(w=2 * D, tok_b=D)
CONST = dict(ident=128, gamma=D, beta=D, causal=128, proxy=PROXIES)
LATER = dict(clip=128, down=PAIRS, be1=CH, bk1=CH, bk2=2, b1=EXPERTS * FCH, gate=EXPERTS,
             gate_b=EXPERTS, be2=D)
ROWS = dict(up=D, b2=D)
MLPW = dict(we1=HIDDEN, wk1=HIDDEN, we2=CH * D, wk2=CH * 2 * D)


def columns(pack):
    at, out = 0, {}
    for name, width in pack.items():
        out[name] = slice(at, at + width)
        at += width
    return out, at


def build(nc, patches_in, first_in, const_in, later_in, rows_in, keyw_in, mlpw_in, w1_in, w2_in, out):
    with ExitStack() as ctx:
        def sb(name, shape):
            return ctx.enter_context(nc.sbuf_tensor(name, shape, F32))

        def bank(name):
            return ctx.enter_context(nc.psum_tensor(name, [128, 512], F32))

        def sem(name):
            return ctx.enter_context(nc.semaphore(name))

        def each(name):
            return [sem(f"{name}{t}") for t in range(TILES)]

        FC, n_first = columns(FIRST)
        CC, n_const = columns(CONST)
        LC, n_later = columns(LATER)
        RC, n_rows = columns(ROWS)
        MC, n_mlpw = columns(MLPW)
        first = sb("first", [128, n_first])
        patches = sb("patches", [128, TILES, 2, 128])
        const = sb("const", [128, n_const])
        later = sb("later", [128, n_later])
        rows = sb("rows", [PAIRS, n_rows])
        keyw = sb("keyw", [128, 2, GHEADS, D + 2 * KEYS])
        mlpw = sb("mlpw", [128, n_mlpw])
        w1 = sb("w1", [128, EXPERTS, FCH, 128])
        w2 = sb("w2", [128, EXPERTS, FCH, D])
        tok_w = first[:, FC["w"]].rearrange("f (c d) -> f c d", c=2)
        ident, gamma, beta = const[:, CC["ident"]], const[:, CC["gamma"]], const[:, CC["beta"]]
        causal, proxy_t = const[:, CC["causal"]], const[:, CC["proxy"]]
        other_clip = later[:, LC["clip"]]
        be1, bk1, bk2, b1 = (later[:, LC[n]] for n in ("be1", "bk1", "bk2", "b1"))
        we1_t, wk1_t = mlpw[:, MC["we1"]], mlpw[:, MC["wk1"]]
        we2_t = mlpw[:, MC["we2"]].rearrange("h (c d) -> h c d", c=CH)
        wk2_t = mlpw[:, MC["wk2"]].rearrange("h (c d) -> h c d", c=CH)

        ones = sb("ones", [1, 128])
        eps = sb("eps", [128, 2])
        proxy_q = sb("proxy_q", [128, PROXIES])
        keymat = sb("keymat", [128, HEADS, 2, KEYS])

        stats = sb("stats", [128, TILES, NORMS, 6])
        mv = sb("mv", [128, TILES, NORMS, 2])
        lnvar = sb("lnvar", [128, TILES, NORMS])
        rstd = sb("rstd", [128, TILES, NORMS])
        centred = sb("centred", [128, TILES, D])
        h = sb("h", [128, TILES, 4, D])
        h_bias = sb("h_bias", [128, TILES, D])
        h_centred = sb("h_centred", [128, D])
        xn = sb("xn", [128, TILES, 4, D])
        xt = sb("xt", [128, TILES, 4, 128])
        negmax = sb("negmax", [128, TILES, 3])
        total = sb("total", [128, TILES, 3])
        inv = sb("inv", [128, TILES, 3])
        mix = sb("mix", [128, TILES, PROXIES])
        prods_t = sb("prods_t", [PROXIES, TILES, 128])
        mix_t = sb("mix_t", [PROXIES, TILES, 128])
        att_t = sb("att_t", [128, TILES, 128])
        scores = sb("scores", [128, TILES, HEADS, 2, KEYS])
        rest = sb("rest", [128, TILES, HEADS, 2, KEYS])
        best = sb("best", [128, TILES, HEADS, 2, TOPK])
        pairs = sb("pairs", [128, TILES, HEADS, PAIRS])
        shifted = sb("shifted", [128, TILES, HEADS, PAIRS])
        expo = sb("expo", [128, TILES, HEADS, PAIRS])
        left8 = sb("left8", [128, TILES, HEADS, PAIRS])
        left16 = sb("left16", [128, TILES, HEADS, PAIRS])
        pair_top = sb("pair_top", [128, TILES, HEADS, TOPK])
        chosen = sb("chosen", [128, TILES, HEADS, PAIRS])
        norm16 = sb("norm16", [128, TILES, HEADS])
        inv16 = sb("inv16", [128, TILES, HEADS])
        taken = sb("taken", [128, TILES, WEIGHED[0][1], PAIRS])
        negbest = sb("negbest", [128, TILES, HEADS])
        top_exp = sb("top_exp", [128, TILES, HEADS, TOPK])
        share = sb("share", [128, TILES, HEADS, PAIRS])
        gelu = sb("gelu", [PAIRS, TILES, 128])
        expert_t = sb("expert_t", [PAIRS, TILES, 128])
        hk = sb("hk", [128, TILES, CH, 128])
        he = sb("he", [128, TILES, CH, 128])
        kq = sb("kq", [128, TILES, 2, 128])
        embs = sb("embs", [128, TILES, D])
        logits = sb("logits", [128, TILES, 128])
        clip_p = sb("clip_p", [128, TILES, 128])
        clip_t = sb("clip_t", [128, TILES, 128])
        gate = sb("gate", [128, TILES, 16])
        gate_top = sb("gate_top", [128, TILES, 8])
        gate_raw = sb("gate_raw", [128, TILES, EXPERTS])
        gate_neg = sb("gate_neg", [128, TILES])
        gate_left = sb("gate_left", [128, TILES, 16])
        gate_exp = sb("gate_exp", [128, TILES, EXPERTS])
        gate_w = sb("gate_w", [128, TILES, EXPERTS])
        gate_t = sb("gate_t", [EXPERTS, TILES, 128])
        hid = sb("hid", [128, TILES, EXPERTS, FCH, 128])
        acc = sb("acc", [128, TILES, EXPERTS + 1, D])
        busy = ctx.enter_context(nc.sbuf_tensor("busy", [128, 256], mybir.dt.bfloat16))

        chain = [bank(f"chain{t}") for t in range(TILES)]
        wide = [bank(f"wide{i}") for i in range(6)]

        patches_s = [sem(f"patches_in{t}") for t in range(TILES)]
        keyw_s = [sem(f"keyw_in{b}") for b in range(2)]
        first_in_s, const_s, later_s, rows_s, mlpw_s, w1_s, w2_s, stored = (
            sem(n) for n in ("first_in", "const_in", "later_in", "rows_in", "mlpw_in",
                             "w1_in", "w2_in", "stored"))
        consts_set, proxy_q_ready, busy_set = sem("consts_set"), sem("proxy_q_ready"), sem("busy_set")
        keymat_done, keymat_ready = sem("keymat_done"), sem("keymat_ready")
        stats_ready, var_ready, lnvar_ready, rstd_ready, h_ready, xn_ready, xt_done, xt_ready = (
            each(n) for n in ("stats_ready", "var_ready", "lnvar_ready", "rstd_ready", "h_ready",
                              "xn_ready", "xt_done", "xt_ready"))
        proj_done, centred_ready = sem("proj_done"), sem("centred_ready")
        (prods_done, prods_t_done, prod_max, prods_t_ready, mix_ready, mix_inv, mix_t_done, mix_t_ready, att_done,
         att_ready, att_out) = (sem(n) for n in (
            "prods_done", "prods_t_done", "prod_max", "prods_t_ready", "mix_ready", "mix_inv", "mix_t_done",
            "mix_t_ready", "att_done", "att_ready", "att_out"))
        (scores_done, down_done, scores_ready, gelu_ready, best8, rest_ready, best16, pairs_ready,
         shifted_ready, expo_ready, pair8, left8_ready, pair16, left16_ready, taken_ready, negbest_ready,
         norm16_ready, inv16_ready, expert_w_done, expert_t_ready, up_done) = (sem(n) for n in (
            "scores_done", "down_done", "scores_ready", "gelu_ready", "best8", "rest_ready",
            "best16", "pairs_ready", "shifted_ready", "expo_ready", "pair8", "left8_ready",
            "pair16", "left16_ready", "taken_ready", "negbest_ready", "norm16_ready", "inv16_ready",
            "expert_w_done", "expert_t_ready", "up_done"))
        chosen_ready = [sem(f"chosen_ready{n}") for n in range(len(WEIGHED))]
        share_ready = [sem(f"share_ready{n}") for n in range(len(WEIGHED))]
        mlp_done = [sem(f"mlp_done{i}") for i in range(3)]
        mlp_ready = [sem(f"mlp_ready{i}") for i in range(3)]
        (key_done, query_done, embs_done, key_ready,
         query_ready, embs_ready, logits_done, logits_ready, logit_max, clip_ready, clip_inv,
         clip_t_done, clip_t_ready, clip_out) = (sem(n) for n in (
            "key_done", "query_done", "embs_done",
            "key_ready", "query_ready", "embs_ready", "logits_done", "logits_ready", "logit_max",
            "clip_ready", "clip_inv", "clip_t_done", "clip_t_ready", "clip_out"))
        (gate_done, gate_ready, gate_sorted, gate_two, gate_neg_ready, gate_left_ready,
         gate_exp_ready, gate_w_ready, gate_sum, gate_inv, gate_t_done, gate_t_ready, b2_done,
         hid_done, hid_ready, expert_done, gate_raw_ready, b2_ready) = (sem(n) for n in (
            "gate_done", "gate_ready", "gate_sorted", "gate_two", "gate_neg_ready",
            "gate_left_ready", "gate_exp_ready", "gate_w_ready", "gate_sum", "gate_inv",
            "gate_t_done", "gate_t_ready", "b2_done", "hid_done", "hid_ready", "expert_done",
            "gate_raw_ready", "b2_ready"))
        acc_ready = each("acc_ready")
        h_centred_ready = sem("h_centred_ready")
        h_bias_ready = sem("h_bias_ready")

        score_bank = [(wide[0], wide[1], wide[4], wide[5], wide[2]),
                      (wide[3], wide[0], wide[1], wide[5], wide[2])]
        fold_bank = [wide[2], wide[3]]
        down_bank = wide[4]
        prods_bank = (wide[4], wide[1])
        mlp_bank = [(wide[4], chain[t], wide[5]) for t in range(TILES)]
        hid_bank = (wide[0], wide[1], wide[4])
        expert_bank = [(wide[2], wide[3]) * 3 + (wide[5], wide[2]),
                       (wide[3], wide[5], wide[2], chain[0]) * 2]

        block = ctx.enter_context(nc.Block())

        @block.sync
        def _(sp):
            sp.dma_start(first[:, :], first_in).then_inc(first_in_s, 16)
            sp.dma_start(patches[:, 1, :, :], patches_in[:, 1, :, :]).then_inc(patches_s[1], 16)
            for b in range(2):
                sp.dma_start(keyw[:, b, :, :], keyw_in[:, b, :, :]).then_inc(keyw_s[b], 16)
            sp.dma_start(later[:, :], later_in).then_inc(later_s, 16)
            sp.dma_start(rows[:, :], rows_in).then_inc(rows_s, 16)
            sp.dma_start(mlpw[:, :], mlpw_in).then_inc(mlpw_s, 16)
            sp.dma_start(w1[:, :, :, :], w1_in).then_inc(w1_s, 16)
            sp.dma_start(w2[:, :, :, :], w2_in).then_inc(w2_s, 16)
            for t in range(TILES):
                sp.wait_ge(acc_ready[t], EXPERTS)
                sp.dma_start(out[t * 128:(t + 1) * 128, :], acc[:, t, EXPERTS, :]).then_inc(stored, 16)
            sp.wait_ge(stored, 16 * TILES)

        @block.gpsimd
        def _(pool):
            pool.memset(ones[:, :], 1.0).then_inc(consts_set, 1)
            pool.memset(eps[:, 0:1], TOK_EPS).then_inc(consts_set, 1)
            pool.memset(eps[:, 1:2], LN_EPS).then_inc(consts_set, 1)
            for t in range(TILES):
                pool.memset(gate[:, t, EXPERTS:16], REMOVED).then_inc(consts_set, 1)

            def build_pairs(t, g):
                hs = slice(g * GHEADS, (g + 1) * GHEADS)
                pool.wait_ge(best16, 2 * HEADS * t + 2 * GHEADS * (g + 1))
                at = 0
                for i0, ni, nj in RECTS:
                    shape = [128, GHEADS, ni, nj]
                    pool.tensor_tensor(
                        pairs[:, t, hs, at:at + ni * nj].rearrange("p h (i j) -> p h i j", j=nj),
                        best[:, t, hs, 0, i0:i0 + ni].unsqueeze(3).to_broadcast(shape),
                        best[:, t, hs, 1, 0:nj].unsqueeze(2).to_broadcast(shape),
                        ALU.add).then_inc(pairs_ready, 1)
                    at += ni * nj
                pool.wait_ge(pairs_ready, len(RECTS) * (GROUPS * t + g + 1))
                pool.tensor_scalar(negbest[:, t, hs], pairs[:, t, hs, 0], -1.0, None,
                                   ALU.mult).then_inc(negbest_ready, 1)
                pool.tensor_tensor(
                    shifted[:, t, hs, :], pairs[:, t, hs, :],
                    pairs[:, t, hs, 0:1].to_broadcast([128, GHEADS, PAIRS]),
                    ALU.subtract).then_inc(shifted_ready, 1)

            def pair_weights(t):
                h0, h1 = WEIGHED[0]
                hs = slice(h0, h1)
                pool.wait_ge(left16_ready, HEADS * t + h1)
                pool.tensor_scalar(taken[:, t, :, :], left16[:, t, hs, :], REMOVED, None,
                                   ALU.is_equal).then_inc(taken_ready, 1)
                pool.wait_ge(taken_ready, t + 1)
                pool.wait_ge(expo_ready, GROUPS * t + (h1 - 1) // GHEADS + 1)
                pool.tensor_tensor(chosen[:, t, hs, :], taken[:, t, :, :], expo[:, t, hs, :],
                                   ALU.mult).then_inc(chosen_ready[0], 1)

            def divide(t, n):
                hs = slice(*WEIGHED[n])
                pool.wait_ge(chosen_ready[n], t + 1)
                pool.wait_ge(inv16_ready, len(WEIGHED) * t + n + 1)
                pool.tensor_tensor(
                    share[:, t, hs, :], chosen[:, t, hs, :],
                    inv16[:, t, hs].unsqueeze(2).to_broadcast([128, hs.stop - hs.start, PAIRS]),
                    ALU.mult).then_inc(share_ready[n], 1)

            def add_value_bias(t):
                if t == 0:
                    pool.wait_ge(later_s, 16)
                pool.wait_ge(h_ready[t], 3)
                pool.tensor_tensor(h_bias[:, t, :], h[:, t, 2, :], later[:, LC["be2"]],
                                   ALU.add).then_inc(h_bias_ready, 1)

            def centre(t, n):
                pool.wait_ge(h_ready[t], n)
                pool.wait_ge(var_ready[t], n + 1)
                pool.tensor_tensor(h_centred[:, :], h[:, t, n - 1, :],
                                   mv[:, t, n, 0:1].to_broadcast([128, D]), ALU.subtract)\
                    .then_inc(h_centred_ready, 1)

            centre(1, 2)
            for t in range(TILES):
                for g in range(GROUPS):
                    build_pairs(t, g)
                pair_weights(t)
                divide(t, 0)
                divide(t, 1)
                add_value_bias(t)

        @block.tensor
        def _(pe):
            def stay_warm(n, bank=wide[5]):
                for _ in range(n):
                    nc.tensor.matmul(bank[:, 0:256], busy[:, 0:128], busy[:, :],
                                     start=True, stop=True)

            def project(t):
                if t == 0:
                    pe.wait_ge(consts_set, 1)
                    pe.wait_ge(first_in_s, 16)
                nc.tensor.matmul(chain[t][:, 0:D], ones[0:1, :], first[0:1, FC["tok_b"]],
                                 start=True, stop=False)
                pe.wait_ge(patches_s[t], 16)
                for c in range(2):
                    last = nc.tensor.matmul(chain[t][:, 0:D], patches[:, t, c, :],
                                            tok_w[:, c, :], start=False, stop=(c == 1))
                last.then_inc(proj_done, 1)

            def fold_keys(h0, n):
                for hd in range(h0, h0 + n):
                    b, g = hd // GHEADS, hd % GHEADS
                    if g == 0:
                        pe.wait_ge(keyw_s[b], 16)
                    nc.tensor.matmul(fold_bank[b][:, g * 2 * KEYS:(g + 1) * 2 * KEYS],
                                     keyw[:, b, g, 0:D], keyw[:, b, g, D:],
                                     start=True, stop=True).then_inc(keymat_done, 1)

            def turn_x(t, n):
                pe.wait_ge(xn_ready[t], n + 1)
                nc.tensor.transpose(chain[t][:, 128:256], xn[:, t, n, :], ident)\
                    .then_inc(xt_done[t], 1)

            def proxy_products(t):
                pe.wait_ge(xt_ready[t], 1)
                if t == 0:
                    pe.wait_ge(proxy_q_ready, 1)
                nc.tensor.matmul(chain[t][:, 256:256 + PROXIES], xt[:, t, 0, :], proxy_q[:, :],
                                 start=True, stop=True).then_inc(prods_done, 1)
                nc.tensor.matmul(prods_bank[t][0:PROXIES, 384:512], proxy_t, xt[:, t, 0, :],
                                 start=True, stop=True).then_inc(prods_t_done, 1)

            def turn_mix(t):
                pe.wait_ge(mix_ready, t + 1)
                nc.tensor.transpose(chain[t][0:PROXIES, 0:128], mix[:, t, :], ident)\
                    .then_inc(mix_t_done, 1)

            def proxy_attention(t):
                pe.wait_ge(prods_t_ready, t + 1)
                pe.wait_ge(mix_t_ready, t + 1)
                nc.tensor.matmul(chain[t][:, 128:256], prods_t[:, t, :], mix_t[:, t, :],
                                 start=True, stop=True).then_inc(att_done, 1)

            def proxy_output(t):
                pe.wait_ge(att_ready, t + 1)
                nc.tensor.matmul(chain[t][:, 256:384], att_t[:, t, :], xn[:, t, 0, :],
                                 start=True, stop=True).then_inc(att_out, 1)

            def key_scores(t):
                pe.wait_ge(xt_ready[t], 2)
                if t == 1:
                    pe.wait_ge(scores_ready, len(SCORED))
                for q, (h0, h1) in enumerate(SCORED):
                    if t == 0:
                        pe.wait_ge(keymat_ready, (h1 - 1) // GHEADS + 1)
                    nc.tensor.matmul(
                        score_bank[t][q][:, 0:(h1 - h0) * 2 * KEYS], xt[:, t, 1, :],
                        keymat[:, h0:h1, :, :].rearrange("f h a k -> f (h a k)"),
                        start=True, stop=True).then_inc(scores_done, 1)

            def down(t):
                if t == 0:
                    pe.wait_ge(later_s, 16)
                    pe.wait_ge(scores_ready, 3)
                pe.wait_ge(xt_ready[t], 2)
                nc.tensor.matmul(down_bank[0:PAIRS, t * 128:(t + 1) * 128], later[:, LC["down"]],
                                 xt[:, t, 1, :], start=True, stop=True).then_inc(down_done, 1)

            def sum_heads(t, n):
                h0, h1 = WEIGHED[n]
                pe.wait_ge(share_ready[n], t + 1)
                for hd in range(h0, h1):
                    last = nc.tensor.matmul(chain[t][0:PAIRS, 0:128], share[:, t, hd, :], ident,
                                            start=(hd == 0), stop=(hd == HEADS - 1))
                if h1 == HEADS:
                    last.then_inc(expert_w_done, 1)

            def expert_up(t):
                pe.wait_ge(expert_t_ready, t + 1)
                if t == 0:
                    pe.wait_ge(rows_s, 16)
                nc.tensor.matmul(chain[t][:, 256:384], expert_t[:, t, :], rows[0:PAIRS, RC["up"]],
                                 start=True, stop=True).then_inc(up_done, 1)

            def mlp_hidden(t):
                pe.wait_ge(xt_ready[t], 3)
                if t == 0:
                    pe.wait_ge(mlpw_s, 16)
                else:
                    pe.wait_ge(hid_ready, 3)
                for i in range(3):
                    units = ((0, 1), (2, 3), (0, 1, 2, 3))[i]
                    for c, u in enumerate(units):
                        last = nc.tensor.matmul(mlp_bank[t][i][:, c * 128:(c + 1) * 128],
                                                (wk1_t, we1_t)[i // 2][:, u * 128:(u + 1) * 128],
                                                xt[:, t, 2, :], start=True, stop=True)
                    last.then_inc(mlp_done[i], 1)

            def keys_queries(t):
                for half, done in enumerate((key_done, query_done)):
                    for c in range(CH):
                        if c % 2 == 0:
                            pe.wait_ge(mlp_ready[c // 2], 2 * (t + 1))
                        last = nc.tensor.matmul(mlp_bank[t][half][:, 0:128],
                                                wk2_t[:, c, half * D:(half + 1) * D],
                                                hk[:, t, c, :], start=(c == 0), stop=(c == CH - 1))
                    last.then_inc(done, 1)

            def values(t, c0, c1):
                if c0 == 0:
                    pe.wait_ge(mlp_ready[2], CH * (t + 1))
                for c in range(c0, c1):
                    last = nc.tensor.matmul(mlp_bank[t][2][:, 0:D], he[:, t, c, :], we2_t[:, c, :],
                                            start=(c == 0), stop=(c == CH - 1))
                if c1 == CH:
                    last.then_inc(embs_done, 1)

            def clip_logits(t):
                pe.wait_ge(key_ready, t + 1)
                pe.wait_ge(query_ready, t + 1)
                nc.tensor.matmul(chain[t][:, 0:128], kq[:, t, 1, :], kq[:, t, 0, :],
                                 start=True, stop=True).then_inc(logits_done, 1)

            def turn_clip(t):
                pe.wait_ge(clip_ready, t + 1)
                nc.tensor.transpose(chain[t][:, 128:256], clip_p[:, t, :], ident)\
                    .then_inc(clip_t_done, 1)

            def clip_output(t):
                pe.wait_ge(clip_t_ready, t + 1)
                pe.wait_ge(embs_ready, t + 1)
                nc.tensor.matmul(chain[t][:, 256:384], clip_t[:, t, :], embs[:, t, :],
                                 start=True, stop=True).then_inc(clip_out, 1)

            def gate_logits(t):
                pe.wait_ge(xt_ready[t], 4)
                nc.tensor.matmul(chain[t][:, 0:EXPERTS], xt[:, t, 3, :], later[:, LC["gate"]],
                                 start=True, stop=True).then_inc(gate_done, 1)

            def expert_hidden(t, e):
                n = EXPERTS * t + e
                if n == 0:
                    pe.wait_ge(w1_s, 16)
                if n >= len(hid_bank):
                    pe.wait_ge(hid_ready, n - len(hid_bank) + 1)
                for f in range(FCH):
                    last = nc.tensor.matmul(hid_bank[n % len(hid_bank)][:, f * 128:(f + 1) * 128],
                                            w1[:, e, f, :], xt[:, t, 3, :], start=True, stop=True)
                last.then_inc(hid_done, 1)

            def expert_output(t, e):
                if t == 0 and e == 0:
                    pe.wait_ge(w2_s, 16)
                to = expert_bank[t][e]
                before = [(p, b) for p in range(t + 1) for b in range(e if p == t else EXPERTS)
                          if expert_bank[p][b] is to]
                if before:
                    pe.wait_ge(acc_ready[before[-1][0]], before[-1][1] + 1)
                elif t == 1:
                    pe.wait_ge(b2_ready, 1)
                pe.wait_ge(hid_ready, EXPERTS * t + e + 1)
                for f in range(FCH):
                    last = nc.tensor.matmul(to[:, 0:D], hid[:, t, e, f, :],
                                            w2[:, e, f, :], start=(f == 0), stop=(f == FCH - 1))
                last.then_inc(expert_done, 1)

            def turn_gate(t):
                pe.wait_ge(gate_w_ready, t + 1)
                nc.tensor.transpose(chain[t][0:EXPERTS, 0:128], gate_w[:, t, :], ident)\
                    .then_inc(gate_t_done, 1)

            def gate_bias(t):
                pe.wait_ge(gate_t_ready, t + 1)
                nc.tensor.matmul(chain[t][:, 384:512], gate_t[:, t, :], rows[0:EXPERTS, RC["b2"]],
                                 start=True, stop=True).then_inc(b2_done, 1)

            pe.wait_ge(busy_set, 1)
            stay_warm(11)
            project(0)
            stay_warm(2)
            project(1)
            stay_warm(8)
            pe.wait_ge(const_s, 16)
            fold_keys(0, 3)
            turn_x(0, 0)
            fold_keys(3, 1)
            proxy_products(0)
            stay_warm(6)
            turn_mix(0)
            turn_x(1, 0)
            stay_warm(2)
            proxy_attention(0)
            proxy_products(1)
            fold_keys(4, 2)
            stay_warm(1)
            proxy_output(0)
            fold_keys(6, 2)
            turn_mix(1)
            stay_warm(2)
            proxy_attention(1)
            stay_warm(4)
            turn_x(0, 1)
            proxy_output(1)
            key_scores(0)
            turn_x(1, 1)
            down(0)
            down(1)
            key_scores(1)
            pe.wait_ge(scores_ready, len(SCORED) * TILES)
            pe.wait_ge(best16, 12)
            stay_warm(30, wide[3])
            sum_heads(0, 0)
            sum_heads(0, 1)
            sum_heads(0, 2)
            stay_warm(3, wide[3])
            expert_up(0)
            stay_warm(21, wide[3])
            turn_x(0, 2)
            stay_warm(3, wide[3])
            mlp_hidden(0)
            keys_queries(0)
            values(0, 0, 2)
            clip_logits(0)
            values(0, 2, CH)
            stay_warm(4, wide[3])
            turn_clip(0)
            stay_warm(3, wide[3])
            clip_output(0)
            stay_warm(9, wide[3])
            sum_heads(1, 0)
            turn_x(0, 3)
            sum_heads(1, 1)
            sum_heads(1, 2)
            gate_logits(0)
            expert_hidden(0, 0)
            expert_up(1)
            expert_hidden(0, 1)
            expert_hidden(0, 2)
            expert_output(0, 0)
            expert_output(0, 1)
            expert_hidden(0, 3)
            turn_x(1, 2)
            expert_output(0, 2)
            mlp_hidden(1)
            keys_queries(1)
            expert_output(0, 3)
            expert_hidden(0, 4)
            clip_logits(1)
            turn_gate(0)
            values(1, 0, CH)
            expert_hidden(0, 5)
            turn_clip(1)
            gate_bias(0)
            expert_output(0, 4)
            clip_output(1)
            expert_hidden(0, 6)
            expert_output(0, 5)
            expert_hidden(0, 7)
            expert_output(0, 6)
            turn_x(1, 3)
            expert_output(0, 7)
            gate_logits(1)
            expert_hidden(1, 0)
            expert_hidden(1, 1)
            expert_hidden(1, 2)
            for e in range(EXPERTS):
                if e + 3 < EXPERTS:
                    expert_hidden(1, e + 3)
                if e == 1:
                    turn_gate(1)
                if e == 2:
                    gate_bias(1)
                expert_output(1, e)

        @block.scalar
        def _(act):
            act.dma_start(patches[:, 0, :, :], patches_in[:, 0, :, :]).then_inc(patches_s[0], 16)
            act.dma_start(const[:, :], const_in).then_inc(const_s, 16)
            nc.scalar.preload_act_table_set("natural_log_exp_and_others")

            def inverse_std(t, n):
                act.wait_ge(var_ready[t], n + 1)
                e = 0 if n == 0 else 1
                nc.scalar.activation(lnvar[:, t, n:n + 1], mv[:, t, n, 1:2], ACT.Ln,
                                     bias=eps[:, e:e + 1]).then_inc(lnvar_ready[t], 1)
                act.wait_ge(lnvar_ready[t], n + 1)
                nc.scalar.activation(rstd[:, t, n:n + 1], lnvar[:, t, n:n + 1], ACT.Exp,
                                     scale=-0.5).then_inc(rstd_ready[t], 1)

            def scale_norm(t, n):
                act.wait_ge(h_centred_ready, 1)
                act.wait_ge(rstd_ready[t], n + 1)
                nc.scalar.activation(xn[:, t, n - 1, :], h_centred[:, :], ACT.Copy,
                                     scale=rstd[:, t, n:n + 1]).then_inc(xn_ready[t], 1)

            def keep_xt(t, n):
                act.wait_ge(xt_done[t], n + 1)
                nc.scalar.activation(xt[:, t, n, :], chain[t][:, 128:256], ACT.Copy)\
                    .then_inc(xt_ready[t], 1)

            def proxy_softmax(t):
                act.wait_ge(prod_max, t + 1)
                nc.scalar.activation(mix[:, t, :], chain[t][:, 256:256 + PROXIES], ACT.Exp,
                                     bias=negmax[:, t, 0:1], accum_out=total[:, t, 0:1])\
                    .then_inc(mix_ready, 1)

            def keep_keymat(b):
                act.wait_ge(keymat_done, GHEADS * (b + 1))
                nc.scalar.activation(
                    keymat[:, b * GHEADS:(b + 1) * GHEADS, :, :].rearrange("f h a k -> f (h a k)"),
                    fold_bank[b][:, :], ACT.Copy).then_inc(keymat_ready, 1)

            def keep_scores(t, q):
                h0, h1 = SCORED[q]
                act.wait_ge(scores_done, len(SCORED) * t + q + 1)
                nc.scalar.activation(
                    scores[:, t, h0:h1, :, :].rearrange("p h a k -> p (h a k)"),
                    score_bank[t][q][:, 0:(h1 - h0) * 2 * KEYS], ACT.Copy).then_inc(scores_ready, 1)

            def expert_gelu(t):
                act.wait_ge(down_done, TILES)
                nc.scalar.activation(gelu[:, t, :], down_bank[0:PAIRS, t * 128:(t + 1) * 128],
                                     ACT.Gelu).then_inc(gelu_ready, 1)

            def pair_exp(t, g):
                act.wait_ge(shifted_ready, GROUPS * t + g + 1)
                hs = slice(g * GHEADS, (g + 1) * GHEADS)
                nc.scalar.activation(expo[:, t, hs, :], shifted[:, t, hs, :], ACT.Exp)\
                    .then_inc(expo_ready, 1)

            def weight_sums(t, h0, h1):
                act.wait_ge(negbest_ready, GROUPS * t + (h1 - 1) // GHEADS + 1)
                for hd in range(h0, h1):
                    act.wait_ge(pair16, HEADS * t + hd + 1)
                    nc.scalar.activation(top_exp[:, t, hd, :], pair_top[:, t, hd, :], ACT.Exp,
                                         bias=negbest[:, t, hd:hd + 1],
                                         accum_out=norm16[:, t, hd:hd + 1])\
                        .then_inc(norm16_ready, 1)

            def mlp_relu(t, i):
                to, bias = ((hk, bk1), (he, be1))[i // 2]
                act.wait_ge(mlp_done[i], t + 1)
                for c, u in enumerate(((0, 1), (2, 3), (0, 1, 2, 3))[i]):
                    nc.scalar.activation(to[:, t, u, :], mlp_bank[t][i][:, c * 128:(c + 1) * 128],
                                         ACT.Relu, bias=bias[:, u:u + 1]).then_inc(mlp_ready[i], 1)

            def keep_keys(t):
                act.wait_ge(key_done, t + 1)
                nc.scalar.activation(kq[:, t, 0, :], mlp_bank[t][0][:, 0:128], ACT.Identity,
                                     bias=bk2[:, 0:1]).then_inc(key_ready, 1)

            def keep_queries(t):
                act.wait_ge(query_done, t + 1)
                nc.scalar.activation(kq[:, t, 1, :], mlp_bank[t][1][:, 0:128], ACT.Identity,
                                     bias=bk2[:, 1:2]).then_inc(query_ready, 1)

            def keep_embs(t):
                act.wait_ge(embs_done, t + 1)
                nc.scalar.activation(embs[:, t, :], mlp_bank[t][2][:, 0:D], ACT.Copy)\
                    .then_inc(embs_ready, 1)

            def clip_softmax(t):
                act.wait_ge(logit_max, t + 1)
                nc.scalar.activation(clip_p[:, t, :], logits[:, t, :], ACT.Exp,
                                     bias=negmax[:, t, 1:2], accum_out=total[:, t, 1:2])\
                    .then_inc(clip_ready, 1)

            def keep_clip_t(t):
                act.wait_ge(clip_t_done, t + 1)
                nc.scalar.activation(clip_t[:, t, :], chain[t][:, 128:256], ACT.Copy)\
                    .then_inc(clip_t_ready, 1)

            def gate_softmax(t):
                act.wait_ge(gate_neg_ready, t + 1)
                nc.scalar.activation(gate_exp[:, t, :], gate[:, t, 0:EXPERTS], ACT.Exp,
                                     bias=gate_neg[:, t:t + 1]).then_inc(gate_exp_ready, 1)

            def keep_gate_t(t):
                act.wait_ge(gate_t_done, t + 1)
                nc.scalar.activation(gate_t[:, t, :], chain[t][0:EXPERTS, 0:128], ACT.Copy)\
                    .then_inc(gate_t_ready, 1)

            def expert_relu(t, e):
                n = EXPERTS * t + e
                act.wait_ge(hid_done, n + 1)
                for f in range(FCH):
                    unit = e * FCH + f
                    last = nc.scalar.activation(
                        hid[:, t, e, f, :], hid_bank[n % len(hid_bank)][:, f * 128:(f + 1) * 128],
                        ACT.Relu, bias=b1[:, unit:unit + 1])
                last.then_inc(hid_ready, 1)

            act.wait_ge(const_s, 16)
            nc.scalar.activation(proxy_q[:, :], proxy_t, ACT.Copy, scale=PROXIES ** -0.5)\
                .then_inc(proxy_q_ready, 1)
            act.wait_ge(consts_set, 3)
            inverse_std(0, 0)
            inverse_std(0, 1)
            inverse_std(1, 0)
            keep_xt(0, 0)
            keep_keymat(0)
            inverse_std(1, 1)
            proxy_softmax(0)
            keep_xt(1, 0)
            proxy_softmax(1)
            inverse_std(0, 2)
            keep_keymat(1)
            keep_xt(0, 1)
            for q in range(len(SCORED)):
                keep_scores(0, q)
            inverse_std(1, 2)
            scale_norm(1, 2)
            keep_xt(1, 1)
            for t in range(TILES):
                expert_gelu(t)
            nc.scalar.preload_act_table_set("natural_log_exp_and_others")
            for q in range(len(SCORED)):
                keep_scores(1, q)
            pair_exp(0, 0)
            pair_exp(0, 1)
            weight_sums(0, 0, HEADS)
            inverse_std(0, 3)
            keep_xt(0, 2)
            for i in range(3):
                mlp_relu(0, i)
            keep_keys(0)
            pair_exp(1, 0)
            keep_queries(0)
            pair_exp(1, 1)
            weight_sums(1, 0, 3)
            clip_softmax(0)
            keep_embs(0)
            keep_clip_t(0)
            weight_sums(1, 3, 6)
            inverse_std(0, 4)
            weight_sums(1, 6, HEADS)
            keep_xt(0, 3)
            expert_relu(0, 0)
            gate_softmax(0)
            expert_relu(0, 1)
            inverse_std(1, 3)
            expert_relu(0, 2)
            keep_xt(1, 2)
            expert_relu(0, 3)
            mlp_relu(1, 0)
            mlp_relu(1, 2)
            keep_keys(1)
            keep_queries(1)
            expert_relu(0, 4)
            keep_gate_t(0)
            clip_softmax(1)
            keep_embs(1)
            keep_clip_t(1)
            expert_relu(0, 5)
            expert_relu(0, 6)
            inverse_std(1, 4)
            expert_relu(0, 7)
            keep_xt(1, 3)
            expert_relu(1, 0)
            gate_softmax(1)
            for e in range(1, EXPERTS):
                expert_relu(1, e)
                if e == 3:
                    keep_gate_t(1)

        @block.vector
        def _(dve):
            dve.memset(busy[:, :], 1.0).then_inc(busy_set, 1)

            def moments(t, n, src):
                nc.vector.bn_stats(stats[:, t, n, :], src).then_inc(stats_ready[t], 1)
                variance(t, n)

            def h_stats(t, n):
                dve.wait_ge(h_ready[t], n)
                nc.vector.bn_stats(stats[:, t, n, :], h[:, t, n - 1, :]).then_inc(stats_ready[t], 1)

            def variance(t, n):
                dve.wait_ge(stats_ready[t], n + 1)
                nc.vector.bn_aggr(mv[:, t, n, :], stats[:, t, n, :]).then_inc(var_ready[t], 1)

            def normalize(t, n):
                dve.wait_ge(rstd_ready[t], n + 1)
                nc.vector.tensor_scalar(xn[:, t, n - 1, :], h[:, t, n - 1, :], mv[:, t, n, 0:1],
                                        rstd[:, t, n:n + 1], ALU.subtract, ALU.mult)\
                    .then_inc(xn_ready[t], 1)

            def token_norm(t):
                dve.wait_ge(proj_done, t + 1)
                moments(t, 0, chain[t][:, 0:D])

            def token_centre(t):
                if t == 0:
                    dve.wait_ge(const_s, 16)
                dve.wait_ge(var_ready[t], 1)
                nc.vector.scalar_tensor_tensor(centred[:, t, :], chain[t][:, 0:D], mv[:, t, 0, 0:1],
                                               gamma, ALU.subtract, ALU.mult)\
                    .then_inc(centred_ready, 1)

            def token_out(t):
                dve.wait_ge(centred_ready, t + 1)
                dve.wait_ge(rstd_ready[t], 1)
                nc.vector.scalar_tensor_tensor(h[:, t, 0, :], centred[:, t, :], rstd[:, t, 0:1],
                                               beta, ALU.mult, ALU.add).then_inc(h_ready[t], 1)

            def h_moments(t, n):
                h_stats(t, n)
                variance(t, n)

            def proxy_max(t):
                dve.wait_ge(prods_done, t + 1)
                nc.vector.tensor_reduce(negmax[:, t, 0:1], chain[t][:, 256:256 + PROXIES],
                                        axis=AX.X, op=ALU.max, negate=True).then_inc(prod_max, 1)

            def keep_prods_t(t):
                dve.wait_ge(prods_t_done, t + 1)
                nc.vector.tensor_copy(prods_t[:, t, :], prods_bank[t][0:PROXIES, 384:512])\
                    .then_inc(prods_t_ready, 1)

            def keep_mix_t(t):
                dve.wait_ge(mix_t_done, t + 1)
                nc.vector.tensor_copy(mix_t[:, t, :], chain[t][0:PROXIES, 0:128])\
                    .then_inc(mix_t_ready, 1)
                nc.vector.reciprocal(inv[:, t, 0:1], total[:, t, 0:1]).then_inc(mix_inv, 1)

            def mask_attention(t):
                dve.wait_ge(att_done, t + 1)
                nc.vector.tensor_tensor(att_t[:, t, :], chain[t][:, 128:256], causal, ALU.mult)\
                    .then_inc(att_ready, 1)

            def add_attention(t):
                dve.wait_ge(att_out, t + 1)
                dve.wait_ge(mix_inv, t + 1)
                nc.vector.scalar_tensor_tensor(h[:, t, 1, :], chain[t][:, 256:384], inv[:, t, 0:1],
                                               h[:, t, 0, :], ALU.mult, ALU.add)\
                    .then_inc(h_ready[t], 1)

            def first_keys(t, hd):
                dve.wait_ge(scores_ready, len(SCORED) * t + sum(h0 <= hd for h0, _ in SCORED))
                for a in range(2):
                    nc.vector.max(best[:, t, hd, a, 0:8], scores[:, t, hd, a, :]).then_inc(best8, 1)

            def strike_keys(t, hd):
                for a in range(2):
                    dve.wait_ge(best8, 2 * HEADS * t + 2 * hd + a + 1)
                    nc.vector.match_replace(rest[:, t, hd, a, :], best[:, t, hd, a, 0:8],
                                            scores[:, t, hd, a, :], REMOVED).then_inc(rest_ready, 1)

            def last_keys(t, hd):
                for a in range(2):
                    dve.wait_ge(rest_ready, 2 * HEADS * t + 2 * hd + a + 1)
                    nc.vector.max(best[:, t, hd, a, 8:16], rest[:, t, hd, a, :]).then_inc(best16, 1)

            def best_keys(t, hd):
                first_keys(t, hd)
                strike_keys(t, hd)
                last_keys(t, hd)

            def first_pairs(t, h0):
                two = (h0, h0 + 1)
                dve.wait_ge(pairs_ready, len(RECTS) * (GROUPS * t + h0 // GHEADS + 1))
                for hd in two:
                    nc.vector.max(pair_top[:, t, hd, 0:8], pairs[:, t, hd, :]).then_inc(pair8, 1)
                for hd in two:
                    dve.wait_ge(pair8, HEADS * t + hd + 1)
                    nc.vector.match_replace(left8[:, t, hd, :], pair_top[:, t, hd, 0:8],
                                            pairs[:, t, hd, :], REMOVED).then_inc(left8_ready, 1)

            def last_pairs(t, h0):
                two = (h0, h0 + 1)
                for hd in two:
                    dve.wait_ge(left8_ready, HEADS * t + hd + 1)
                    nc.vector.max(pair_top[:, t, hd, 8:16], left8[:, t, hd, :]).then_inc(pair16, 1)
                for hd in two:
                    dve.wait_ge(pair16, HEADS * t + hd + 1)
                    nc.vector.match_replace(left16[:, t, hd, :], pair_top[:, t, hd, 8:16],
                                            left8[:, t, hd, :], REMOVED).then_inc(left16_ready, 1)

            def best_pairs(t, h0):
                first_pairs(t, h0)
                last_pairs(t, h0)

            def pair_weights(t, n):
                h0, h1 = WEIGHED[n]
                hs = slice(h0, h1)
                dve.wait_ge(left16_ready, HEADS * t + h1)
                dve.wait_ge(expo_ready, GROUPS * t + (h1 - 1) // GHEADS + 1)
                nc.vector.scalar_tensor_tensor(chosen[:, t, hs, :], left16[:, t, hs, :], REMOVED,
                                               expo[:, t, hs, :], ALU.is_equal, ALU.mult)\
                    .then_inc(chosen_ready[n], 1)

            def weight_inverse(t, n):
                h0, h1 = WEIGHED[n]
                dve.wait_ge(norm16_ready, HEADS * t + h1)
                nc.vector.reciprocal(inv16[:, t, h0:h1], norm16[:, t, h0:h1]).then_inc(inv16_ready, 1)

            def divide(t, n):
                hs = slice(*WEIGHED[n])
                dve.wait_ge(chosen_ready[n], t + 1)
                dve.wait_ge(inv16_ready, len(WEIGHED) * t + n + 1)
                nc.vector.tensor_tensor(
                    share[:, t, hs, :], chosen[:, t, hs, :],
                    inv16[:, t, hs].unsqueeze(2).to_broadcast([128, hs.stop - hs.start, PAIRS]),
                    ALU.mult).then_inc(share_ready[n], 1)

            def expert_mix(t):
                dve.wait_ge(expert_w_done, t + 1)
                if t == 0:
                    dve.wait_ge(gelu_ready, TILES)
                nc.vector.tensor_tensor(expert_t[:, t, :], chain[t][0:PAIRS, 0:128], gelu[:, t, :],
                                        ALU.mult).then_inc(expert_t_ready, 1)

            def add_experts(t):
                dve.wait_ge(up_done, t + 1)
                nc.vector.tensor_tensor(h[:, t, 2, :], chain[t][:, 256:384], h[:, t, 1, :], ALU.add)\
                    .then_inc(h_ready[t], 1)

            def mlp_relu():
                dve.wait_ge(mlp_done[1], 2)
                for c, u in enumerate((2, 3)):
                    nc.vector.tensor_scalar(hk[:, 1, u, :], mlp_bank[1][1][:, c * 128:(c + 1) * 128],
                                            bk1[:, u:u + 1], 0.0, ALU.add, ALU.max)\
                        .then_inc(mlp_ready[1], 1)

            def clip_max(t):
                dve.wait_ge(logits_done, t + 1)
                nc.vector.tensor_tensor(logits[:, t, :], chain[t][:, 0:128], other_clip, ALU.add)\
                    .then_inc(logits_ready, 1)
                dve.wait_ge(logits_ready, t + 1)
                nc.vector.tensor_reduce(negmax[:, t, 1:2], logits[:, t, :], axis=AX.X, op=ALU.max,
                                        negate=True).then_inc(logit_max, 1)

            def clip_inverse(t):
                dve.wait_ge(clip_ready, t + 1)
                nc.vector.reciprocal(inv[:, t, 1:2], total[:, t, 1:2]).then_inc(clip_inv, 1)

            def add_clip(t):
                dve.wait_ge(clip_out, t + 1)
                dve.wait_ge(clip_inv, t + 1)
                dve.wait_ge(h_bias_ready, t + 1)
                nc.vector.scalar_tensor_tensor(h[:, t, 3, :], chain[t][:, 256:384], inv[:, t, 1:2],
                                               h_bias[:, t, :], ALU.mult, ALU.add)\
                    .then_inc(h_ready[t], 1)

            def gate_copy(t):
                dve.wait_ge(gate_done, t + 1)
                nc.vector.tensor_tensor(gate[:, t, 0:EXPERTS], chain[t][:, 0:EXPERTS],
                                        later[:, LC["gate_b"]], ALU.add)\
                    .then_inc(gate_ready, 1)

            def gate_order(t):
                dve.wait_ge(gate_ready, t + 1)
                nc.vector.max(gate_top[:, t, :], gate[:, t, :]).then_inc(gate_sorted, 1)

            def gate_strike(t):
                dve.wait_ge(gate_sorted, t + 1)
                nc.vector.tensor_scalar(gate_neg[:, t:t + 1], gate_top[:, t, 0:1], -1.0, None,
                                        ALU.mult).then_inc(gate_neg_ready, 1)
                nc.vector.memset(gate_top[:, t, 2:8], REMOVED).then_inc(gate_two, 1)

            def gate_mark(t):
                dve.wait_ge(gate_two, t + 1)
                nc.vector.match_replace(gate_left[:, t, :], gate_top[:, t, :], gate[:, t, :], TAKEN)\
                    .then_inc(gate_left_ready, 1)
                dve.wait_ge(gate_left_ready, t + 1)
                dve.wait_ge(gate_exp_ready, t + 1)
                nc.vector.scalar_tensor_tensor(gate_raw[:, t, :], gate_left[:, t, 0:EXPERTS], TAKEN,
                                               gate_exp[:, t, :], ALU.is_equal, ALU.mult)\
                    .then_inc(gate_raw_ready, 1)

            def gate_total(t):
                dve.wait_ge(gate_raw_ready, t + 1)
                nc.vector.tensor_reduce(total[:, t, 2:3], gate_raw[:, t, :], axis=AX.X, op=ALU.add)\
                    .then_inc(gate_sum, 1)

            def gate_inverse(t):
                dve.wait_ge(gate_sum, t + 1)
                nc.vector.reciprocal(inv[:, t, 2:3], total[:, t, 2:3]).then_inc(gate_inv, 1)

            def gate_scale(t):
                dve.wait_ge(gate_inv, t + 1)
                nc.vector.tensor_scalar(gate_w[:, t, :], gate_raw[:, t, :], inv[:, t, 2:3], None,
                                        ALU.mult).then_inc(gate_w_ready, 1)

            def add_expert(t, e):
                dve.wait_ge(expert_done, EXPERTS * t + e + 1)
                before = acc[:, t, e, :]
                if e == 0:
                    dve.wait_ge(gate_w_ready, t + 1)
                    before = h[:, t, 3, :]
                elif e == BIASES_AT[t]:
                    dve.wait_ge(b2_ready, t + 1)
                    before = acc[:, t, 0, :]
                else:
                    dve.wait_ge(acc_ready[t], e)
                nc.vector.scalar_tensor_tensor(acc[:, t, e + 1, :], expert_bank[t][e][:, 0:D],
                                               gate_w[:, t, e:e + 1], before, ALU.mult, ALU.add)\
                    .then_inc(acc_ready[t], 1)

            def add_biases(t):
                dve.wait_ge(b2_done, t + 1)
                dve.wait_ge(acc_ready[t], BIASES_AT[t])
                nc.vector.tensor_tensor(acc[:, t, 0, :], chain[t][:, 384:512],
                                        acc[:, t, BIASES_AT[t], :],
                                        ALU.add).then_inc(b2_ready, 1)

            token_norm(0)
            token_centre(0)
            token_out(0)
            h_moments(0, 1)
            token_norm(1)
            normalize(0, 1)
            token_centre(1)
            token_out(1)
            h_moments(1, 1)
            proxy_max(0)
            keep_prods_t(0)
            normalize(1, 1)
            keep_mix_t(0)
            mask_attention(0)
            proxy_max(1)
            keep_prods_t(1)
            add_attention(0)
            h_stats(0, 2)
            variance(0, 2)
            keep_mix_t(1)
            normalize(0, 2)
            mask_attention(1)
            add_attention(1)
            h_stats(1, 2)
            best_keys(0, 0)
            variance(1, 2)
            best_keys(0, 1)
            best_keys(0, 2)
            for hd in range(3, HEADS):
                best_keys(0, hd)
            best_pairs(0, 0)
            best_pairs(0, 2)
            best_pairs(0, 4)
            first_pairs(0, 6)
            weight_inverse(0, 0)
            pair_weights(0, 1)
            last_pairs(0, 6)
            weight_inverse(0, 1)
            pair_weights(0, 2)
            first_keys(1, 0)
            weight_inverse(0, 2)
            strike_keys(1, 0)
            divide(0, 2)
            last_keys(1, 0)
            best_keys(1, 1)
            expert_mix(0)
            best_keys(1, 2)
            add_experts(0)
            first_keys(1, 3)
            h_stats(0, 3)
            strike_keys(1, 3)
            variance(0, 3)
            last_keys(1, 3)
            first_keys(1, 4)
            normalize(0, 3)
            strike_keys(1, 4)
            last_keys(1, 4)
            for hd in range(5, HEADS):
                best_keys(1, hd)
            best_pairs(1, 0)
            best_pairs(1, 2)
            first_pairs(1, 4)
            clip_max(0)
            last_pairs(1, 4)
            clip_inverse(0)
            pair_weights(1, 1)
            first_pairs(1, 6)
            add_clip(0)
            weight_inverse(1, 0)
            h_stats(0, 4)
            variance(0, 4)
            last_pairs(1, 6)
            weight_inverse(1, 1)
            pair_weights(1, 2)
            normalize(0, 4)
            weight_inverse(1, 2)
            divide(1, 2)
            expert_mix(1)
            gate_copy(0)
            gate_order(0)
            gate_strike(0)
            add_experts(1)
            h_stats(1, 3)
            gate_mark(0)
            variance(1, 3)
            gate_total(0)
            gate_inverse(0)
            gate_scale(0)
            normalize(1, 3)
            add_expert(0, 0)
            add_expert(0, 1)
            mlp_relu()
            add_expert(0, 2)
            clip_max(1)
            add_expert(0, 3)
            clip_inverse(1)
            add_clip(1)
            h_stats(1, 4)
            variance(1, 4)
            add_expert(0, 4)
            add_biases(0)
            normalize(1, 4)
            add_expert(0, 5)
            add_expert(0, 6)
            gate_copy(1)
            gate_order(1)
            gate_strike(1)
            add_expert(0, 7)
            gate_mark(1)
            gate_total(1)
            gate_inverse(1)
            gate_scale(1)
            for e in range(EXPERTS):
                if e == BIASES_AT[1]:
                    add_biases(1)
                add_expert(1, e)


def kernel(**inputs):
    import numpy as np
    import concourse.bacc as bacc
    from concourse.bass_utils import run_bass_kernel_spmd as run

    a = {k: np.asarray(v) for k, v in inputs.items()}

    def pack(layout, parts, height=128):
        where, width = columns(layout)
        out = np.zeros((height, width), np.float32)
        for name, part in parts.items():
            out[:part.shape[0], where[name]] = part
        return out

    def by_column(v):
        return v.reshape(-1, 128).T

    token = np.arange(128)
    same_clip = token[:, None] // PATCHES == token[None, :] // PATCHES
    cells = np.concatenate([(np.arange(i0, i0 + ni)[:, None] * TOPK + np.arange(nj)).ravel()
                            for i0, ni, nj in RECTS])
    keys = np.zeros((2, DKEY, HEADS, 2, KEYS), np.float32)
    for p in range(2):
        keys[p, :, :, p, :] = a["L0_ffn_keys"][:, :, p, :].transpose(2, 0, 1)
    wq = a["L0_ffn_W_q"].reshape(D, 2, HEADS, DKEY).transpose(1, 3, 2, 0)
    x = a["x"].reshape(CLIPS, -1)
    patches = np.stack([x[:, p * BLOCK:(p + 2) * BLOCK] for p in range(PATCHES)], axis=1)
    arrays = {
        "patches": np.ascontiguousarray(
            patches.reshape(TILES, 128, 2, 128).transpose(3, 0, 2, 1)),
        "first": pack(FIRST, {
            "w": a["L0_tok_W"].reshape(2, 128, D).transpose(1, 0, 2).reshape(128, -1),
            "tok_b": a["L0_tok_b"][None]}),
        "const": pack(CONST, {
            "ident": np.eye(128, dtype=np.float32),
            "gamma": np.broadcast_to(a["L0_tok_gamma"], (128, D)),
            "beta": np.broadcast_to(a["L0_tok_beta"], (128, D)),
            "causal": (same_clip & (token[:, None] <= token[None, :])).astype(np.float32),
            "proxy": a["L0_attn_proxy"].T}),
        "later": pack(LATER, {
            "clip": np.where(same_clip, 0.0, -1e30).astype(np.float32),
            "down": a["L0_ffn_down_embed"][cells].T,
            "be1": by_column(a["L1_attn_be1"]), "bk1": by_column(a["L1_attn_bk1"]),
            "bk2": by_column(a["L1_attn_bk2"]), "b1": by_column(a["L1_ffn_b1"]),
            "gate": a["L1_ffn_gate_w"],
            "gate_b": np.broadcast_to(a["L1_ffn_gate_b"], (128, EXPERTS)),
            "be2": np.broadcast_to(a["L1_attn_be2"], (128, D))}),
        "rows": pack(ROWS, {
            "up": a["L0_ffn_up_embed"][cells], "b2": a["L1_ffn_b2"]}, PAIRS),
        "keyw": np.concatenate([wq.reshape(128, HEADS, D), keys.reshape(128, HEADS, 2 * KEYS)], axis=2)
        .reshape(128, 2, GHEADS, D + 2 * KEYS),
        "mlpw": pack(MLPW, {
            "we1": a["L1_attn_We1"].T, "wk1": a["L1_attn_Wk1"].T,
            "we2": a["L1_attn_We2"].T.reshape(CH, 128, D).transpose(1, 0, 2).reshape(128, -1),
            "wk2": a["L1_attn_Wk2"].T.reshape(CH, 128, 2 * D).transpose(1, 0, 2).reshape(128, -1)}),
        "w1": np.ascontiguousarray(a["L1_ffn_w1"].reshape(EXPERTS, D, FCH, 128).transpose(1, 0, 2, 3)),
        "w2": np.ascontiguousarray(a["L1_ffn_w2"].reshape(EXPERTS, FCH, 128, D).transpose(2, 0, 1, 3)),
    }
    nc = bacc.Bacc("TRN2", target_bir_lowering=False, num_devices=1)
    args = [nc.dram_tensor(f"{n}_dram", v.shape, mybir.dt.from_np(v.dtype), kind="ExternalInput").ap()
            for n, v in arrays.items()]
    out = nc.dram_tensor("out_dram", (CLIPS, PATCHES, D), F32, kind="ExternalOutput").ap()
    build(nc, *args, out.rearrange("b p d -> (b p) d"))
    r = run(nc, [{f"{n}_dram": v for n, v in arrays.items()}], core_ids=[0])
    return r.results[0]["out_dram"]
```
